# Optimizing a Trainium2 kernel written in Bass

```python
import numpy as np
import jax
import jax.numpy as jnp

def _softmax(x, axis=-1):
    return jax.nn.softmax(x, axis=axis)

def _gelu(x):
    return jax.nn.gelu(x, approximate=True)

def _silu(x):
    return jax.nn.silu(x)

def _sigmoid(x):
    return jax.nn.sigmoid(x)

def _layernorm(x, axis=-1, eps=1e-05):
    m = jnp.mean(x, axis=axis, keepdims=True)
    v = jnp.var(x, axis=axis, keepdims=True)
    return (x - m) / jnp.sqrt(v + eps)

def _scatter_add(tgt, idx, src, axis=0):
    return tgt.at[idx].add(src)

def _segment_sum(src, seg, n):
    return jax.ops.segment_sum(src, seg, n)
kernel_name = 'mk_gnn_resnorm_d2_gnn_r8_7a89f3'

def setup_inputs(seed: int=0):
    np.random.seed(seed)
    _w = jnp.asarray

    def _rec_inputs():
        import jax
        import jax.numpy as jnp
        _gk = jax.random.key(seed)
        x = -0.000202 + 1 * jax.random.normal(jax.random.fold_in(_gk, 1), (12500, 64), jnp.float32)
        src = jax.random.randint(jax.random.fold_in(_gk, 2), (400000,), 0, 12500, jnp.int32)
        dst = jnp.minimum((12500 * jax.random.uniform(jax.random.fold_in(_gk, 3), (400000,)) ** 2.0).astype(jnp.int32), 99999)
        _o = jnp.argsort(dst, stable=True)
        src = src[_o]
        dst = dst[_o]
        edge_attr_64 = -5.16925e-05 + 1.00005 * jax.random.normal(jax.random.fold_in(_gk, 12), (400000, 64), jnp.float32)
        return (x, src, dst, edge_attr_64)
    x, src, dst, edge_attr_64 = _rec_inputs()

    def _L0_gnn_setup():
        import jax, jax.numpy as jnp
        import numpy as np
        N, E, D_IN, D_OUT = (12500, 100000, 64, 64)
        key = jax.random.key(seed)
        k_x, k_s, k_d, k_w1, k_b1, k_w2, k_b2 = jax.random.split(key, 7)
        x = jax.random.normal(k_x, (N, D_IN), dtype=jnp.float32)
        src = jax.random.randint(k_s, (E,), 0, N, dtype=jnp.int32)
        dst = jax.random.randint(k_d, (E,), 0, N, dtype=jnp.int32)
        s1 = 1.0 / np.sqrt(2 * D_IN)
        W_fc = jax.random.uniform(k_w1, (2 * D_IN, D_OUT), minval=-s1, maxval=s1, dtype=jnp.float32)
        b_fc = jax.random.uniform(k_b1, (D_OUT,), minval=-s1, maxval=s1, dtype=jnp.float32)
        s2 = 1.0 / np.sqrt(D_IN)
        W_res = jax.random.uniform(k_w2, (D_IN, D_OUT), minval=-s2, maxval=s2, dtype=jnp.float32)
        b_res = jax.random.uniform(k_b2, (D_OUT,), minval=-s2, maxval=s2, dtype=jnp.float32)
        return {'x': x, 'src': src, 'dst': dst, 'W_fc': W_fc, 'b_fc': b_fc, 'W_res': W_res, 'b_res': b_res}
    _L0_gnn_all = _L0_gnn_setup()
    _L0_gnn_in = {k: v for k, v in _L0_gnn_all.items() if k in ('W_fc', 'b_fc', 'W_res', 'b_res')}
    del _L0_gnn_all

    def _L1_gnn_setup():
        import jax, jax.numpy as jnp
        import numpy as np
        N_NODES = 12500
        N_EDGES = 200000
        D = 64

        def _general_conv(x, edge_attr, src, dst, Wm, bm, We, be, Ws, bs):
            msg = x[src] @ Wm + bm + edge_attr @ We + be
            agg = jax.ops.segment_sum(msg, dst, num_segments=x.shape[0])
            return agg + x @ Ws + bs
        key = jax.random.key(seed)
        ks = jax.random.split(key, 16)
        s = 1.0 / np.sqrt(D)
        x = jax.random.normal(ks[0], (N_NODES, D), dtype=jnp.float32)
        edge_index = jax.random.randint(ks[1], (2, N_EDGES), 0, N_NODES, dtype=jnp.int64)
        edge_attr = jax.random.normal(ks[2], (N_EDGES, D), dtype=jnp.float32)
        p = {}
        names = ['Wm1', 'We1', 'Ws1', 'Wm2', 'We2', 'Ws2']
        for i, n in enumerate(names):
            p[n] = jax.random.normal(ks[3 + i], (D, D), dtype=jnp.float32) * s
        for n in ['bm1', 'be1', 'bs1', 'bm2', 'be2', 'bs2']:
            p[n] = jnp.zeros((D,), dtype=jnp.float32)
        return {'x': x, 'edge_index': edge_index, 'edge_attr': edge_attr, **p}
    _L1_gnn_all = _L1_gnn_setup()
    _L1_gnn_in = {k: v for k, v in _L1_gnn_all.items() if k in ('Wm1', 'bm1', 'We1', 'be1', 'Ws1', 'bs1', 'Wm2', 'bm2', 'We2', 'be2', 'Ws2', 'bs2')}
    del _L1_gnn_all
    return {'x': x, 'src': src, 'dst': dst, 'edge_attr_64': edge_attr_64, 'L0_gnn_W_fc': _L0_gnn_in['W_fc'], 'L0_gnn_b_fc': _L0_gnn_in['b_fc'], 'L0_gnn_W_res': _L0_gnn_in['W_res'], 'L0_gnn_b_res': _L0_gnn_in['b_res'], 'L1_gnn_Wm1': _L1_gnn_in['Wm1'], 'L1_gnn_bm1': _L1_gnn_in['bm1'], 'L1_gnn_We1': _L1_gnn_in['We1'], 'L1_gnn_be1': _L1_gnn_in['be1'], 'L1_gnn_Ws1': _L1_gnn_in['Ws1'], 'L1_gnn_bs1': _L1_gnn_in['bs1'], 'L1_gnn_Wm2': _L1_gnn_in['Wm2'], 'L1_gnn_bm2': _L1_gnn_in['bm2'], 'L1_gnn_We2': _L1_gnn_in['We2'], 'L1_gnn_be2': _L1_gnn_in['be2'], 'L1_gnn_Ws2': _L1_gnn_in['Ws2'], 'L1_gnn_bs2': _L1_gnn_in['bs2']}

def reference(x, src, dst, edge_attr_64, L0_gnn_W_fc, L0_gnn_b_fc, L0_gnn_W_res, L0_gnn_b_res, L1_gnn_Wm1, L1_gnn_bm1, L1_gnn_We1, L1_gnn_be1, L1_gnn_Ws1, L1_gnn_bs1, L1_gnn_Wm2, L1_gnn_bm2, L1_gnn_We2, L1_gnn_be2, L1_gnn_Ws2, L1_gnn_bs2):
    import jax
    import jax.numpy as jnp

    def _L0_gnn_ref(x, src, dst, W_fc, b_fc, W_res, b_res):
        import jax, jax.numpy as jnp
        import numpy as np
        N, E, D_IN, D_OUT = (12500, 100000, 64, 64)
        n = x.shape[0]
        agg = jax.ops.segment_sum(x[src], dst, num_segments=n)
        deg = jax.ops.segment_sum(jnp.ones_like(dst, dtype=x.dtype), dst, num_segments=n)
        mean = agg / jnp.maximum(deg, 1.0)[:, None]
        h = jnp.concatenate([x, mean], axis=-1) @ W_fc + b_fc
        h = jax.nn.relu(h)
        h = h + x @ W_res + b_res
        return h

    def _L1_gnn_ref(x, edge_index, edge_attr, Wm1, bm1, We1, be1, Ws1, bs1, Wm2, bm2, We2, be2, Ws2, bs2):
        import jax, jax.numpy as jnp
        import numpy as np
        N_NODES = 12500
        N_EDGES = 200000
        D = 64

        def _general_conv(x, edge_attr, src, dst, Wm, bm, We, be, Ws, bs):
            msg = x[src] @ Wm + bm + edge_attr @ We + be
            agg = jax.ops.segment_sum(msg, dst, num_segments=x.shape[0])
            return agg + x @ Ws + bs
        src, dst = (edge_index[0], edge_index[1])
        h = _general_conv(x, edge_attr, src, dst, Wm1, bm1, We1, be1, Ws1, bs1)
        h = jax.nn.relu(h)
        out = _general_conv(h, edge_attr, src, dst, Wm2, bm2, We2, be2, Ws2, bs2)
        return out
    edge_index = jnp.stack([src, dst])
    x = _layernorm(x + _L0_gnn_ref(x, src, dst, L0_gnn_W_fc, L0_gnn_b_fc, L0_gnn_W_res, L0_gnn_b_res), axis=-1)
    x = _layernorm(x + _L1_gnn_ref(x, edge_index, edge_attr_64, L1_gnn_Wm1, L1_gnn_bm1, L1_gnn_We1, L1_gnn_be1, L1_gnn_Ws1, L1_gnn_bs1, L1_gnn_Wm2, L1_gnn_bm2, L1_gnn_We2, L1_gnn_be2, L1_gnn_Ws2, L1_gnn_bs2), axis=-1)
    return x

_drawn_inputs = setup_inputs


def setup_inputs(seed=0):
    import zlib

    import numpy as np

    out = dict(_drawn_inputs(seed))
    spreads = {'L1_gnn_bm1': (0.0, 0.1),
     'L1_gnn_be1': (0.0, 0.1),
     'L1_gnn_bs1': (0.0, 0.62),
     'L1_gnn_bm2': (0.0, 0.363),
     'L1_gnn_be2': (0.0, 0.325),
     'L1_gnn_bs2': (0.0, 0.8)}
    factors = {}
    for name, (base, spread) in spreads.items():
        noise = np.random.default_rng([zlib.crc32(name.encode()), seed]).standard_normal(out[name].shape)
        drawn = base * np.exp(spread * noise) if base else spread * noise
        out[name] = jnp.asarray(drawn.astype(out[name].dtype))
    for name, factor in factors.items():
        out[name] = (out[name] * factor).astype(out[name].dtype)
    return out
```

```python
from contextlib import ExitStack

import concourse.bass as bass
from concourse import mybir

F32 = mybir.dt.float32
I32 = mybir.dt.int32
ALU = mybir.AluOpType
ACT = mybir.ActivationFunctionType
ENG = mybir.EngineType
AX = mybir.AxisListType

P = 128
EPS = 1e-5


def gnn_program(nc, x, src, dst, edge_attr, W_fc, b_fc, W_res, b_res,
                Wm1, bm1, We1, be1, Ws1, bs1, Wm2, bm2, We2, be2, Ws2, bs2, out):
    N, D = x.shape
    E = src.shape[0]
    TILES = E // P
    BLOCKS = -(-N // P)
    FULL, REST = N // P, N % P
    NPAD = BLOCKS * P
    STEPS = TILES + BLOCKS - 1
    G = 8
    NG = 4
    ITERS = -(-STEPS // (G * NG))
    SG = -(-ITERS * G * NG // P)
    SPAD = SG * P
    TP = 125
    TC = TILES // TP
    FAR = 1.0e6
    assert TILES * P == E and TP * TC == TILES and 0 < REST < P and BLOCKS % 2 == 0

    ctx = ExitStack()
    with ctx:
        def sb(name, shape, dt=F32):
            return ctx.enter_context(nc.sbuf_tensor(name, shape, dt))

        def sem(name):
            return ctx.enter_context(nc.semaphore(name))

        def sems(name, n):
            return [sem(f"{name}{i}") for i in range(n)]

        x_pad = nc.dram_tensor("x_pad", [NPAD, D], F32).ap()
        x1_tab = nc.dram_tensor("x1_tab", [NPAD, D], F32).ap()
        h_tab = nc.dram_tensor("h_tab", [NPAD, D], F32).ap()
        leave_dram = nc.dram_tensor("leave_dram", [TILES], F32).ap()
        path_dram = nc.dram_tensor("path_dram", [2, SPAD], I32).ap()

        sums = sb("sums", [P, NPAD])
        code = sb("code", [P, SPAD])
        srcn = sb("srcn", [P, SPAD])
        msg = sb("msg", [P, NG * G, 2 * D])
        hot = sb("hot", [P, NG * G, P])
        idx = sb("idx", [P, NG * G], I32)
        xa = sb("xa", [P, BLOCKS, D])
        xb = sb("xb", [P, BLOCKS, D])
        ident = sb("ident", [P, P])
        lane = sb("lane", [P, P])
        ones = sb("ones", [P, 1])
        zpad = sb("zpad", [P - REST, D])
        path = sb("path", [1, 2, SPAD], I32)
        deg = sb("deg", [P, BLOCKS])
        rdeg = sb("rdeg", [P, BLOCKS])
        mean = sb("mean", [P, BLOCKS])
        var = sb("var", [P, BLOCKS])
        rstd = sb("rstd", [P, BLOCKS])
        sdev = sb("sdev", [P, BLOCKS])
        epst = sb("epst", [P, 1])
        tile_no = sb("tile_no", [TP, TC])
        leave = sb("leave", [TP, TC])
        blk = sb("blk", [TP, TC], I32)
        step_no = sb("step_no", [P, SG])
        left = sb("left", [P, SG])
        tb = sb("tb", [P, 2, 32])
        tidx = sb("tidx", [P, SG], I32)
        shift = sb("shift", [P, SG])
        past = sb("past", [P, SG])
        tbT = sb("tbT", [64, P], I32)
        wa = sb("wa", [D + 1, 2 * D])
        wbot = sb("wbot", [D, D])
        wme = [sb(f"wme{i}", [2 * D, D]) for i in range(2)]
        ws = [sb(f"ws{i}", [D + 1, D]) for i in range(2)]
        bme = [sb(f"bme{i}", [P, 2, D]) for i in range(2)]
        cur = sb("cur", [P, 2, D])
        curT = sb("curT", [D + 1, 2, P])
        blkT = sb("blkT", [P, 2, P])
        tmp = sb("tmp", [P, 3, D])
        dst_tm = xa[:, :, :].rearrange("p b d -> p (b d)")[0:TP, 0:TC * P].bitcast(I32)
        leave_all = xb[:, :, :].rearrange("p b d -> p (b d)")[:, 0:TILES]
        junk = xb[:, :, :].rearrange("p b d -> p (b d)")[:, TILES:2 * TILES]
        srows = msg[:, :, :].rearrange("p s d -> p (s d)")[:, 0:SPAD].bitcast(I32)
        drows = hot[:, :, :].rearrange("p s d -> p (s d)")[:, 0:SPAD].bitcast(I32)
        srcf = xa[:, :, :].rearrange("p b d -> p (b d)")[:, 0:SPAD]
        relf = sums[:, 0:SPAD]

        ps = ctx.enter_context(nc.psum_tensor("ps", [P, 8, 512], F32))

        s_const = sem("s_const")
        s_dst_in = sem("s_dst_in")
        s_w = sem("s_w")
        s_xpad = sem("s_xpad")
        s_prep = sem("s_prep")
        s_leave = sem("s_leave")
        s_leave_in = sem("s_leave_in")
        s_srows = sem("s_srows")
        s_drows = sem("s_drows")
        s_prT = sem("s_prT")
        s_prC = sem("s_prC")
        s_path = sem("s_path")
        s_path_in = sem("s_path_in")
        s_zero = sem("s_zero")
        staged = [sems(f"staged{r}_", NG) for r in range(3)]
        claimed = [sem(f"claimed{r}") for r in range(3)]
        gathered = [sems(f"gathered{r}_", NG) for r in range(3)]
        ea_in = sems("ea_in", NG)
        marked = [sems(f"marked{r}_", NG) for r in range(3)]
        summed = [sems(f"summed{r}_", NG) for r in range(3)]
        added = [sems(f"added{r}_", NG) for r in range(3)]
        rows_in = [sems(f"rows_in{r}_", 2) for r in range(3)]
        turning = [sem(f"turning{r}") for r in range(3)]
        turned = [sems(f"turned{r}_", 2) for r in range(3)]
        copied = [sems(f"copied{r}_", 2) for r in range(3)]
        mixed = [sems(f"mixed{r}_", 2) for r in range(3)]
        block_done = [sems(f"block_done{r}_", 2) for r in range(3)]
        s_link = [sem(f"s_link{r}") for r in range(3)]
        s_sqrt = sem("s_sqrt")
        s_norm = sem("s_norm")
        s_store = sems("s_store", 3)

        block = ctx.enter_context(nc.Block())

        def group_cols(i, q):
            return bass.ds(i * (G * NG) + q * G, G)

        @block.sync
        def _(sp):
            sp.dma_start(dst_tm, dst.rearrange("(p t e) -> p (t e)", p=TP, e=P)).then_inc(s_dst_in, 16)
            loads = [(wa[0:D, 0:D], W_fc[0:D, :]), (wa[0:D, D:2 * D], W_res),
                     (wa[D:D + 1, 0:D], b_fc.rearrange("(a n) -> a n", a=1)),
                     (wa[D:D + 1, D:2 * D], b_res.rearrange("(a n) -> a n", a=1)),
                     (wbot[:, :], W_fc[D:2 * D, :])]
            for c, (wm, we, s_, bm, be, bs) in enumerate(((Wm1, We1, Ws1, bm1, be1, bs1),
                                                          (Wm2, We2, Ws2, bm2, be2, bs2))):
                loads += [(wme[c][0:D, :], wm), (wme[c][D:2 * D, :], we), (ws[c][0:D, :], s_),
                          (ws[c][D:D + 1, :], bs.rearrange("(a n) -> a n", a=1)),
                          (bme[c][:, 0, :], bm.rearrange("(a n) -> a n", a=1).to_broadcast([P, D])),
                          (bme[c][:, 1, :], be.rearrange("(a n) -> a n", a=1).to_broadcast([P, D]))]
            assert len(loads) == LOADS
            for to, frm in loads:
                sp.dma_start(to, frm).then_inc(s_w, 16)
            sp.dma_start(x_pad[0:N, :], x).then_inc(s_xpad, 16)
            sp.wait_ge(s_const, 1)
            sp.dma_start(x_pad[N:NPAD, :], zpad[:, :]).then_inc(s_xpad, 16)
            sp.wait_ge(s_prep, LEAVE_DONE)
            sp.dma_start(leave_dram.rearrange("(p t) -> p t", p=TP), leave[:, :]).then_inc(s_leave, 16)
            sp.wait_ge(s_leave, 16)
            sp.dma_start(leave_all, leave_dram.rearrange("(a t) -> a t", a=1).to_broadcast([P, TILES]))\
              .then_inc(s_leave_in, 16)
            sp.wait_ge(s_prC, TB_COPIED)
            for j in range(2):
                sp.dma_start(path_dram[j].rearrange("(g p) -> g p", p=P), tbT[32 * j:32 * j + SG, :])\
                  .then_inc(s_path, 16)
            sp.wait_ge(s_path, 32)
            sp.dma_start(path[:, :, :], path_dram.rearrange("(a j) s -> a j s", a=1)).then_inc(s_path_in, 16)
            sp.wait_ge(s_path_in, 16)
            ea = edge_attr.rearrange("(t e) d -> t e d", e=P)
            sp.wait_ge(s_prC, PREP_COPIED)
            with sp.Fori(0, ITERS) as i:
                for q in range(NG):
                    _, tiles = nc.values_load_multi_w_load_instructions(
                        path[0:1, 0, group_cols(i, q)], engines=(ENG.SP,), min_val=0, max_val=TILES - 1,
                        skip_runtime_bounds_check_because="clamped to TILES - 1 when the path was made")
                    sp.wait_ge(summed[0][q], i * 2 + 1)
                    for k in range(G):
                        sp.dma_start(msg[:, q * G + k, D:2 * D],
                                     ea[bass.ds(tiles[k], 1), :, :].rearrange("t e d -> (t e) d"))\
                          .then_inc(ea_in[q], 16)
            for r, table in enumerate((x_pad, x1_tab, h_tab)):
                rows = table.rearrange("(b p) d -> b p d", p=P)
                if r == 0:
                    sp.wait_ge(s_xpad, 32)
                else:
                    sp.wait_ge(s_store[r - 1], 16)
                with sp.Fori(0, BLOCKS // 2) as i:
                    for h in range(2):
                        sp.wait_ge(block_done[r][h], i + 1)
                        sp.dma_start(cur[:, h, :], rows[bass.ds(i * 2 + h, 1), :, :]
                                     .rearrange("b p d -> (b p) d")).then_inc(rows_in[r][h], 16)
                if r == 0:
                    sp.wait_ge(s_norm, NORMED)
                    sp.dma_start(x1_tab.rearrange("(b p) d -> p b d", p=P), xa[:, :, :]).then_inc(s_store[0], 16)
                elif r == 1:
                    for h in range(2):
                        sp.wait_ge(block_done[1][h], BLOCKS // 2 + 1)
                    sp.dma_start(h_tab.rearrange("(b p) d -> p b d", p=P), xb[:, :, :]).then_inc(s_store[1], 16)
                else:
                    sp.wait_ge(s_norm, 2 * NORMED)
                    sp.dma_start(out[0:FULL * P, :].rearrange("(b p) d -> p b d", p=P), xa[:, 0:FULL, :])\
                      .then_inc(s_store[2], 16)
                    sp.dma_start(out[FULL * P:N, :], xa[0:REST, FULL, :]).then_inc(s_store[2], 16)
                    sp.wait_ge(s_store[2], 32)

        @block.gpsimd
        def _(pool):
            pool.memset(zpad[:, :], 0.0).then_inc(s_const, 1)
            pool.memset(ident[:, :], 0.0).then_inc(s_const, 1)
            pool.iota(tile_no[:, :], [[1, TC]], base=0, channel_multiplier=TC,
                      allow_small_or_imprecise_dtypes=True).then_inc(s_const, 1)
            pool.iota(step_no[:, :], [[P, SG]], base=0, channel_multiplier=1,
                      allow_small_or_imprecise_dtypes=True).then_inc(s_const, 1)
            pool.iota(lane[:, :], [[1, P]], base=0, channel_multiplier=0,
                      allow_small_or_imprecise_dtypes=True).then_inc(s_const, 1)
            pool.memset(ones[:, :], 1.0).then_inc(s_const, 1)
            pool.memset(epst[:, :], EPS).then_inc(s_const, 1)
            pool.wait_ge(s_const, 2)
            pool.affine_select(out=ident[:, :], in_=ident[:, :], compare_op=ALU.not_equal, fill=1.0,
                               base=0, pattern=[[-1, P]], channel_multiplier=1).then_inc(s_const, 1)
            pool.wait_ge(s_prep, PATH_DONE)
            for g in range(SG):
                at = bass.IndirectOffsetOnAxis(ap=tidx[:, g:g + 1], axis=0)
                pool.indirect_dma_start(drows[:, g * P:(g + 1) * P], None,
                                        dst.rearrange("(t e) -> t e", e=P), at).then_inc(s_drows, 16)
            for g in range(SG):
                at = bass.IndirectOffsetOnAxis(ap=tidx[:, g:g + 1], axis=0)
                pool.indirect_dma_start(srows[:, g * P:(g + 1) * P], None,
                                        src.rearrange("(t e) -> t e", e=P), at).then_inc(s_srows, 16)
            for r, table in enumerate((x, x1_tab, h_tab)):
                if r == 0:
                    pool.wait_ge(s_prC, PREP_COPIED)
                else:
                    pool.wait_ge(s_store[r - 1], 16)
                with pool.Fori(0, ITERS) as i:
                    for q in range(NG):
                        pool.wait_ge(staged[r][q], i + 1)
                        pool.sem_inc(claimed[r], 1)
                        for k in range(G):
                            s = q * G + k
                            pool.indirect_dma_start(msg[:, s, 0:D], None, table,
                                                    bass.IndirectOffsetOnAxis(ap=idx[:, s:s + 1], axis=0))\
                                .then_inc(gathered[r][q], 16)

        @block.tensor
        def _(pe):
            for free in [*(x for r in range(3) for x in summed[r] + mixed[r])]:
                pe.sem_inc(free, 1)
            pe.wait_ge(s_const, CONSTS)
            pe.wait_ge(s_prep, PATH_DONE)
            pe.transpose(ps[0:64, 7, 0:P], tb[:, :, :].rearrange("p j g -> p (j g)"), ident[:, :])\
              .then_inc(s_prT, 1)
            n = 0
            for which, ready in ((relf, REL_DONE), (srcf, SRC_DONE)):
                pe.wait_ge(s_prep, ready)
                for g0 in range(0, SG, 4):
                    gs = range(g0, min(g0 + 4, SG))
                    if n >= 4:
                        pe.wait_ge(s_prC, 1 + n - 3)
                    for g in gs:
                        last = pe.transpose(ps[:, n % 4, (g - g0) * P:(g - g0 + 1) * P],
                                            which[:, g * P:(g + 1) * P], ident[:, :])
                    last.then_inc(s_prT, 1)
                    n += 1
            pe.wait_ge(s_prC, PREP_COPIED)
            pe.wait_ge(s_w, 16 * LOADS)
            for r in range(3):
                M = 2 * D if r == 0 else D
                with pe.Fori(0, ITERS) as i:
                    for q in range(NG):
                        pe.wait_ge(marked[r][q], i + 1)
                        pe.wait_ge(gathered[r][q], (i + 1) * (16 * G))
                        if r == 0:
                            pe.wait_ge(ea_in[q], (i + 1) * (16 * G))
                        if q >= 2:
                            pe.wait_ge(added[r][q - 2], i * G + (G + 1))
                        else:
                            pe.wait_ge(added[r][q + 2], i * G + 1)
                        for k in range(G):
                            s = q * G + k
                            bank, col = 2 * (q % 2) + k // 4, k % 4
                            if r == 0:
                                nc.tensor.matmul(ps[:, 4 + bank, col:col + 1], hot[:, s, :], ones[:, :],
                                                 start=True, stop=True)
                            last = nc.tensor.matmul(ps[0:M, bank, col * P:(col + 1) * P],
                                                    msg[:, s, 0:M], hot[:, s, :], start=True, stop=True)
                            if k % 4 == 3:
                                last.then_inc(summed[r][q], 1)
                with pe.Fori(0, BLOCKS // 2) as i:
                    for h in range(2):
                        pe.wait_ge(rows_in[r][h], i * 16 + 16)
                        pe.sem_inc(turning[r], 1)
                        pe.transpose(ps[0:D, h, 0:P], cur[:, h, :], ident[:, :]).then_inc(turned[r][h], 1)
                        pe.wait_ge(copied[r][h], i * 2 + 2)
                        pe.wait_ge(block_done[r][h], i + 1)
                        if r == 0:
                            nc.tensor.matmul(ps[:, 2 + h, 0:2 * D], curT[:, h, :], wa[:, :], start=True, stop=True)
                            nc.tensor.matmul(ps[:, 4 + h, 0:D], blkT[0:D, h, :], wbot[:, :],
                                             start=True, stop=True).then_inc(mixed[r][h], 1)
                        else:
                            nc.tensor.matmul(ps[:, 2 + h, 0:D], blkT[:, h, :], wme[r - 1][:, :],
                                             start=True, stop=False)
                            nc.tensor.matmul(ps[:, 2 + h, 0:D], curT[:, h, :], ws[r - 1][:, :],
                                             start=False, stop=True).then_inc(mixed[r][h], 1)

        @block.scalar
        def _(act):
            act.wait_ge(s_prT, 1)
            act.activation(tbT[:, :], ps[0:64, 7, 0:P], ACT.Copy).then_inc(s_prC, 1)
            n = 0
            for which in (code, srcn):
                for g0 in range(0, SG, 4):
                    g1 = min(g0 + 4, SG)
                    act.wait_ge(s_prT, n + 2)
                    act.activation(which[:, g0 * P:g1 * P], ps[:, n % 4, 0:(g1 - g0) * P], ACT.Copy)\
                       .then_inc(s_prC, 1)
                    n += 1
            act.wait_ge(s_prC, PREP_COPIED)
            for r in range(3):
                with act.Fori(0, ITERS) as i:
                    for q in range(NG):
                        act.wait_ge(summed[r][q], i * 2 + 1)
                        nc.scalar.activation(idx[:, q * G:(q + 1) * G], srcn[:, group_cols(i, q)], ACT.Copy)\
                            .then_inc(staged[r][q], 1)
                for q in range(NG):
                    act.wait_ge(added[r][q], ITERS * G + 1)
                with act.Fori(0, BLOCKS // 2) as i:
                    for h in range(2):
                        act.wait_ge(mixed[r][h], i + 1)
                        nc.scalar.activation(blkT[:, h, :], sums[:, bass.ds((i * 2 + h) * P, P)], ACT.Copy)\
                            .then_inc(copied[r][h], 1)
                        act.wait_ge(turned[r][h], i + 1)
                        nc.scalar.activation(curT[0:D, h, :], ps[0:D, h, 0:P], ACT.Copy).then_inc(copied[r][h], 1)
                if r != 1:
                    act.wait_ge(s_norm, (r // 2) * NORMED + 5)
                    nc.scalar.activation(sdev[:, :], var[:, :], ACT.Sqrt, bias=epst[:, :], scale=1.0 / D)\
                        .then_inc(s_sqrt, 1)

        @block.vector
        def _(dve):
            count = [0]

            def prep(ins):
                count[0] += 1
                ins.then_inc(s_prep, 1)
                dve.wait_ge(s_prep, count[0])

            for free in [*(x for r in range(3) for x in added[r] + block_done[r])]:
                dve.sem_inc(free, 1)
            dve.wait_ge(s_dst_in, 16)
            dve.wait_ge(s_const, CONSTS)
            prep(nc.vector.tensor_single_scalar(blk[:, :], dst_tm.rearrange("p (t e) -> p t e", e=P)[:, :, P - 1],
                                                P.bit_length() - 1, op=ALU.arith_shift_right))
            prep(nc.vector.tensor_tensor(leave[:, :], blk[:, :], tile_no[:, :], ALU.add))
            assert count[0] == LEAVE_DONE
            dve.wait_ge(s_leave_in, 16)
            for g in range(SG):
                prep(nc.vector.tensor_scalar(junk, leave_all, step_no[:, g:g + 1], 0.0, ALU.is_lt, ALU.add,
                                             accum_out=left[:, g:g + 1]))
            prep(nc.vector.memset(tb[:, :, :], 0.0))
            prep(nc.vector.tensor_scalar(tb[:, 0, 0:SG], left[:, :], float(TILES - 1), None, ALU.min))
            prep(nc.vector.tensor_copy(tidx[:, :], tb[:, 0, 0:SG]))
            prep(nc.vector.tensor_tensor(tb[:, 1, 0:SG], step_no[:, :], left[:, :], ALU.subtract))
            prep(nc.vector.tensor_scalar(tb[:, 1, 0:SG], tb[:, 1, 0:SG], float(BLOCKS - 1), None, ALU.min))
            prep(nc.vector.tensor_scalar(past[:, :], left[:, :], float(TILES), -FAR, ALU.is_ge, ALU.mult))
            prep(nc.vector.scalar_tensor_tensor(shift[:, :], tb[:, 1, 0:SG], float(P), past[:, :],
                                                ALU.mult, ALU.add))
            assert count[0] == PATH_DONE, count[0]
            dve.wait_ge(s_drows, 16 * SG)
            prep(nc.vector.tensor_tensor(relf.rearrange("p (g e) -> p g e", e=P),
                                         drows.rearrange("p (g e) -> p g e", e=P),
                                         shift[:, :].unsqueeze(2).to_broadcast([P, SG, P]), ALU.subtract))
            assert count[0] == REL_DONE
            dve.wait_ge(s_srows, 16 * SG)
            prep(nc.vector.tensor_copy(srcf, srows))
            assert count[0] == SRC_DONE
            prep(nc.vector.memset(deg[:, :], 0.0))
            prep(nc.vector.memset(curT[D:D + 1, :, :], 1.0))
            dve.wait_ge(s_w, 16 * LOADS)
            for c in range(2):
                prep(nc.vector.tensor_tensor(bme[c][:, 0, :], bme[c][:, 0, :], bme[c][:, 1, :], ALU.add))
            dve.wait_ge(s_path_in, 16)
            dve.wait_ge(s_prC, PREP_COPIED)
            for r in range(3):
                M = 2 * D if r == 0 else D
                nc.vector.memset(sums[0:M, :], 0.0).then_inc(s_zero, 1)
                dve.wait_ge(s_zero, r + 1)
                with dve.Fori(0, ITERS) as i:
                    for q in range(NG):
                        dve.wait_ge(summed[r][q], i * 2 + 1)
                        nc.vector.tensor_tensor(
                            hot[:, q * G:(q + 1) * G, :],
                            code[:, group_cols(i, q)].unsqueeze(2).to_broadcast([P, G, P]),
                            lane[:, :].unsqueeze(1).to_broadcast([P, G, P]), ALU.is_equal)\
                            .then_inc(marked[r][q], 1)
                        _, blocks = nc.values_load_multi_w_load_instructions(
                            path[0:1, 1, group_cols(i, q)], engines=(ENG.DVE,), min_val=0, max_val=BLOCKS - 1,
                            skip_runtime_bounds_check_because="clamped to BLOCKS - 1 when the path was made")
                        for k in range(G):
                            if k % 4 == 0:
                                dve.wait_ge(summed[r][q], i * 2 + (k // 4 + 2))
                            if k:
                                dve.wait_ge(added[r][q], i * G + (k + 1))
                            elif q:
                                dve.wait_ge(added[r][q - 1], i * G + (G + 1))
                            else:
                                dve.wait_ge(added[r][NG - 1], i * G + 1)
                            b = blocks[k]
                            bank, col = 2 * (q % 2) + k // 4, k % 4
                            if r == 0:
                                nc.vector.tensor_tensor(deg[:, bass.ds(b, 1)], deg[:, bass.ds(b, 1)],
                                                        ps[:, 4 + bank, col:col + 1], ALU.add)
                            at = sums[0:M, bass.ds(b * P, P)]
                            nc.vector.tensor_tensor(
                                at, at, ps[0:M, bank, col * P:(col + 1) * P], ALU.add)\
                                .then_inc(added[r][q], 1)
                for q in range(NG):
                    dve.wait_ge(added[r][q], ITERS * G + 1)

                linked = [0]
                if r == 0:
                    nc.vector.tensor_scalar(rdeg[:, :], deg[:, :], 1.0, None, ALU.max).then_inc(s_link[0], 1)
                    dve.wait_ge(s_link[0], 1)
                    nc.vector.reciprocal(rdeg[:, :], rdeg[:, :]).then_inc(s_link[0], 1)
                    dve.wait_ge(s_link[0], 2)
                    linked[0] = 2
                PER = (3, 1, 1)[r]
                base = linked[0]
                with dve.Fori(0, BLOCKS // 2) as i:
                    for h in range(2):
                        b = i * 2 + h
                        dve.wait_ge(mixed[r][h], i + 2)
                        n = [0]

                        def link(ins):
                            n[0] += 1
                            ins.then_inc(s_link[r], 1)
                            dve.wait_ge(s_link[r], i * (2 * PER) + (h * PER + n[0] + base))

                        if r == 0:
                            link(nc.vector.tensor_scalar(tmp[:, 0, :], ps[:, 4 + h, 0:D], rdeg[:, bass.ds(b, 1)],
                                                         None, ALU.mult))
                            link(nc.vector.tensor_tensor(tmp[:, 1, :], tmp[:, 0, :], ps[:, 2 + h, 0:D], ALU.add))
                            link(nc.vector.scalar_tensor_tensor(tmp[:, 2, :], tmp[:, 1, :], 0.0,
                                                                ps[:, 2 + h, D:2 * D], ALU.max, ALU.add))
                            z = xa[:, bass.ds(b, 1), :].rearrange("p b d -> p (b d)")
                            nc.vector.tensor_tensor(z, tmp[:, 2, :], cur[:, h, :], ALU.add)\
                                .then_inc(block_done[r][h], 1)
                        elif r == 1:
                            link(nc.vector.scalar_tensor_tensor(tmp[:, h, :], bme[0][:, 0, :], deg[:, bass.ds(b, 1)],
                                                                ps[:, 2 + h, 0:D], ALU.mult, ALU.add))
                            nc.vector.tensor_scalar(xb[:, bass.ds(b, 1), :].rearrange("p b d -> p (b d)"),
                                                    tmp[:, h, :], 0.0, None, ALU.max).then_inc(block_done[r][h], 1)
                        else:
                            z = xa[:, bass.ds(b, 1), :].rearrange("p b d -> p (b d)")
                            link(nc.vector.scalar_tensor_tensor(tmp[:, h, :], bme[1][:, 0, :], deg[:, bass.ds(b, 1)],
                                                                ps[:, 2 + h, 0:D], ALU.mult, ALU.add))
                            nc.vector.tensor_tensor(z, tmp[:, h, :], z, ALU.add).then_inc(block_done[r][h], 1)
                if r != 1:
                    dve.wait_ge(block_done[r][0], BLOCKS // 2 + 1)
                    dve.wait_ge(block_done[r][1], BLOCKS // 2 + 1)
                    if r == 0:
                        norms = [0]

                    def norm(ins):
                        norms[0] += 1
                        ins.then_inc(s_norm, 1)
                        dve.wait_ge(s_norm, norms[0])

                    norm(nc.vector.tensor_reduce(mean[:, :], xa[:, :, :], AX.X, ALU.add))
                    norm(nc.vector.tensor_scalar(mean[:, :], mean[:, :], 1.0 / D, None, ALU.mult))
                    norm(nc.vector.tensor_tensor(xa[:, :, :], xa[:, :, :],
                                                 mean[:, :].unsqueeze(2).to_broadcast([P, BLOCKS, D]),
                                                 ALU.subtract))
                    norm(nc.vector.tensor_tensor(xb[:, :, :], xa[:, :, :], xa[:, :, :], ALU.mult))
                    norm(nc.vector.tensor_reduce(var[:, :], xb[:, :, :], AX.X, ALU.add))
                    dve.wait_ge(s_sqrt, r // 2 + 1)
                    norm(nc.vector.reciprocal(rstd[:, :], sdev[:, :]))
                    norm(nc.vector.tensor_tensor(xa[:, :, :], xa[:, :, :],
                                                 rstd[:, :].unsqueeze(2).to_broadcast([P, BLOCKS, D]), ALU.mult))


CONSTS = 8
LOADS = 17
STEP_COLS = 26
LEAVE_DONE = 2
PATH_DONE = LEAVE_DONE + STEP_COLS + 7
REL_DONE = PATH_DONE + 1
SRC_DONE = PATH_DONE + 2
TB_COPIED = 1
PREP_COPIED = 1 + 2 * (-(-STEP_COLS // 4))
NORMED = 7


_INS = ['x', 'src', 'dst', 'edge_attr_64', 'L0_gnn_W_fc', 'L0_gnn_b_fc', 'L0_gnn_W_res', 'L0_gnn_b_res',
        'L1_gnn_Wm1', 'L1_gnn_bm1', 'L1_gnn_We1', 'L1_gnn_be1', 'L1_gnn_Ws1', 'L1_gnn_bs1',
        'L1_gnn_Wm2', 'L1_gnn_bm2', 'L1_gnn_We2', 'L1_gnn_be2', 'L1_gnn_Ws2', 'L1_gnn_bs2']
_OUTS = [((12500, 64), 'float32')]


def kernel(**inputs):
    import numpy as _np
    import concourse.bacc as _bacc
    from concourse import mybir as _mybir
    from concourse.bass_utils import run_bass_kernel_spmd as _run

    nc = _bacc.Bacc("TRN2", target_bir_lowering=False, num_devices=1)
    arrays, args = {}, []
    for name in _INS:
        a = _np.ascontiguousarray(inputs[name])
        arrays[f"in_{name}_dram"] = a
        args.append(nc.dram_tensor(f"in_{name}_dram", a.shape, _mybir.dt.from_np(a.dtype), kind="ExternalInput").ap())
    for i, (shape, dtype) in enumerate(_OUTS):
        dt = _mybir.dt.from_np(_np.dtype(dtype))
        args.append(nc.dram_tensor(f"out_{i}_dram", shape, dt, kind="ExternalOutput").ap())
    gnn_program(nc, *args)
    r = _run(nc, [arrays], core_ids=[0])
    return r.results[0]["out_0_dram"]
```

```python
from contextlib import ExitStack

import concourse.bass as bass
from concourse import mybir

F32 = mybir.dt.float32
F16 = mybir.dt.float16
BF16 = mybir.dt.bfloat16
I32 = mybir.dt.int32
I16 = mybir.dt.int16
ALU = mybir.AluOpType
ACT = mybir.ActivationFunctionType
ENG = mybir.EngineType
AX = mybir.AxisListType

P = 128
EPS = 1e-5
WD = 4
N_NODES, N_EDGES = 12500, 400000
BLOCKS = -(-N_NODES // P)
REGIONS = ((4, 3), (8, 2), (36, 1))
WPB = P // WD


def regions():
    found, step = [], 0
    for n, (b, k) in enumerate(REGIONS):
        end = REGIONS[n + 1][0] if n + 1 < len(REGIONS) else BLOCKS
        found.append((b - REGIONS[0][0], end - b, k, step))
        step += (end - b) * WPB * k
    return found, step


def step_constants():
    import numpy as np
    found, steps = regions()
    cols = -(-steps // P)
    first = np.full(cols * P, 1.0e6, np.float32)
    offset = np.zeros(cols * P, np.float32)
    for b0, blocks, k, s0 in found:
        q = np.arange(blocks * WPB * k)
        first[s0 + q] = (REGIONS[0][0] + b0) * P + q // k * WD
        offset[s0 + q] = q % k * P
    return np.ascontiguousarray(np.stack([first.reshape(cols, P).T, offset.reshape(cols, P).T], axis=1))


def gnn_program(nc, step_c, x, src, dst, edge_attr, W_fc, b_fc, W_res, b_res,
                Wm1, bm1, We1, be1, Ws1, bs1, Wm2, bm2, We2, be2, Ws2, bs2, out):
    N, D = x.shape
    E = src.shape[0]
    assert (N, E) == (N_NODES, N_EDGES)
    T = E // P
    FULL, REST = N // P, N % P
    NPAD = BLOCKS * P
    B0 = REGIONS[0][0]
    DB = BLOCKS - B0
    ITERS = DB // 2
    D0 = B0 * P
    REG, CSTEPS = regions()
    CG = -(-CSTEPS // P)
    HIS = BLOCKS
    WIN = HIS * WD
    HALF = HIS // 2
    G = 8
    SG = -(-(T + BLOCKS - 1) // P)
    SPAD = SG * P
    BESIDE = DB * G
    TP, TC = 125, T // 125
    EG = 5
    GROUPS = T // EG
    EB = 4
    ESTEPS = -(-(GROUPS + BLOCKS - 1) // EB) * EB
    ES = -(-(ESTEPS + 1) // P)
    NB = 7
    NITER = BLOCKS // NB
    F1 = D + 1
    FAR = 1.0e6
    CW = CG * P
    UNION = 2 * CW + 8 * (P + WIN)
    PATH = SPAD + 2 * ES * P + P
    MORE = (SPAD - BESIDE) // (2 * G)
    BG, BC = -(-SG // 4), -(-CG // 4)
    BE = -(-TC // 4)
    assert TP * TC == T and GROUPS * EG == T and BLOCKS % NB == 0
    assert UNION >= (BLOCKS + 2 * G) * 3 * D // 2
    assert all(n % 2 == 0 for _, n, _, _ in REG) and HIS % 2 == 0 and SPAD >= T + BLOCKS - 1 + 2 * G

    ctx = ExitStack()
    with ctx:
        def sb(name, shape, dt=F32):
            return ctx.enter_context(nc.sbuf_tensor(name, shape, dt))

        def sem(name):
            return ctx.enter_context(nc.semaphore(name))

        def sems(name, n):
            return [sem(f"{name}{i}") for i in range(n)]

        x_pad = nc.dram_tensor("x_pad", [NPAD, D], F32).ap()
        x1_tab = nc.dram_tensor("x1_tab", [NPAD, D], F32).ap()
        y_tab = nc.dram_tensor("y_tab", [NPAD, 3 * D], BF16).ap()
        a_dram = [nc.dram_tensor(f"a_dram{j}", [ITERS, 2, P, HALF * P], F16).ap() for j in range(2)]
        left_dram = nc.dram_tensor("left_dram", [T, P], F32).ap()
        last_dram = nc.dram_tensor("last_dram", [T], I32).ap()
        need_dram = nc.dram_tensor("need_dram", [T], F32).ap()
        path_dram = nc.dram_tensor("path_dram", [PATH], I16).ap()
        base_dram = nc.dram_tensor("base_dram", [ES * P], F32).ap()

        acc = sb("acc", [P, BLOCKS, D])
        eas = sb("eas", [P, BLOCKS, F1])
        abuf = sb("abuf", [P, 2, HIS * P], F16)
        union = sb("union", [P, UNION])
        code_g = sb("code_g", [P, SPAD])
        src_g = sb("src_g", [P, SPAD])
        path = sb("path", [1, PATH], I16)
        base_e = sb("base_e", [P, ES * P])
        ident = sb("ident", [P, P])
        lane16 = sb("lane16", [P, WIN], F16)
        lanef = sb("lanef", [P, P])
        epst = sb("epst", [P, 1])
        zpad = sb("zpad", [P - REST, D])
        idx = sb("idx", [P, 2 * G], I32)
        hot_g = sb("hot_g", [P, 2 * G, P], F16)
        part_g = sb("part_g", [P, G, D])
        part_d = sb("part_d", [P, 2, D])
        step_no = sb("step_no", [P, SG])
        sc = sb("sc", [P, 2, CG])
        small = sb("small", [P, 16, CG])
        gidx = sb("gidx", [P, 3, CG], I32)
        rdeg = sb("rdeg", [P, BLOCKS])
        w_in = sb("w_in", [F1, 2, D])
        w_y = sb("w_y", [D, 3, D])
        w_s = sb("w_s", [F1, 2, D])
        w_e = sb("w_e", [D, 2, D])
        bme = sb("bme", [P, 2, 2, D])
        mean = sb("mean", [P, NB])
        sdev = sb("sdev", [P, NB])
        ps = ctx.enter_context(nc.psum_tensor("ps", [P, 8, 512], F32))

        af = abuf[:, :, :].rearrange("p a c -> p (a c)").bitcast(F32)
        accf = acc[:, :, :].rearrange("p b d -> p (b d)")
        easf = eas[:, :, :].rearrange("p b d -> p (b d)")
        smallf = small[:, :, :].rearrange("p a b -> p (a b)")
        code_h, code_l = union[:, 0:CW], union[:, CW:2 * CW]
        hot_c = union[:, 2 * CW:2 * CW + 8 * (WIN + P)].bitcast(F16).rearrange("p (s c) -> p s c", s=16)
        YW = BLOCKS * 3 * D // 2
        yparts = union[:, 0:YW].bitcast(BF16).rearrange("p (b c d) -> p b c d", c=3, d=D)
        ycols = union[:, 0:YW].bitcast(BF16).rearrange("p (b c) -> p b c", c=3 * D)
        msg = union[:, YW:YW + G * 3 * D].bitcast(BF16).rearrange("p (s c) -> p s c", c=3 * D)
        TW = TC * P
        dtf = [*(af[0:TP, k * TW:(k + 1) * TW] for k in range(3)), union[0:TP, 0:TW]]
        dtm = [t.bitcast(I32) for t in dtf]
        wtm = accf[0:TP, 0:TW].bitcast(I32)
        unc = easf[0:TP, 0:TW]
        needt = easf[0:TP, TW:TW + TC]
        lastt = easf[0:TP, TW + TC:TW + 2 * TC].bitcast(I32)
        last_b = af[:, 0:T].bitcast(I32)
        leave_b, taken_b, need_b = (af[:, k * T:(k + 1) * T] for k in (1, 2, 3))
        junk, lastf_b = accf[:, 0:T], accf[:, T:2 * T]
        junk2, leave_e = easf[:, 0:T], easf[:, T:T + GROUPS]
        rows_gd, rows_gs = af[:, 0:SPAD], af[:, SPAD:2 * SPAD].bitcast(I32)
        rows_ct = af[:, 2 * SPAD:2 * SPAD + CW].bitcast(I32)
        rows_cd, rows_cs = af[:, 0:CW].bitcast(I32), af[:, CW:2 * CW].bitcast(I32)
        at = [0]

        def carve(n):
            at[0] += n
            assert at[0] <= HIS * P
            return af[:, at[0] - n:at[0]]

        dst_e = carve(EG * GROUPS).rearrange("p (g j) -> p g j", j=EG)
        dst_rows = carve(TW)[0:TP, :]
        feats = carve(EB * EG * D).rearrange("p (s j d) -> p s j d", s=EB, d=D)
        rests = carve(EB * EG * D).rearrange("p (s j d) -> p s j d", s=EB, d=D)
        EPW = -(-EG * 3 * F1 // 2)
        parts = [carve(EPW).bitcast(BF16)[:, 0:EG * 3 * F1] for _ in range(EB)]
        parts4 = [v.rearrange("p (j c d) -> p j c d", c=3, d=F1) for v in parts]
        parts3 = [v.rearrange("p (j c) -> p j c", c=3 * F1) for v in parts]
        hot_e = carve(EB * EG * P // 2).bitcast(F16).rearrange("p (s j c) -> p s j c", s=EB, c=P)
        rel_e = carve(EB * EG).rearrange("p (s j) -> p s j", s=EB)
        part_e = carve(EB * F1).rearrange("p (s d) -> p s d", s=EB)
        nrow = af[:, 0:NB * D].rearrange("p (b d) -> p b d", d=D)
        feat = af[:, NB * D:2 * NB * D].rearrange("p (b d) -> p b d", d=D)
        t2 = af[:, 2 * NB * D:3 * NB * D].rearrange("p (b d) -> p b d", d=D)
        xT = af[0:F1, 3 * NB * D:3 * NB * D + NB * P]
        eT = af[0:D, 3 * NB * D + NB * P:3 * NB * D + 2 * NB * P]
        ecopy = af[:, 3 * NB * D + 2 * NB * P:4 * NB * D + 2 * NB * P].rearrange("p (b d) -> p b d", d=D)
        regs = smallf[:, 11 * CG:11 * CG + 64]
        trT = sb("trT", [64, P], I16)[:, :]
        trF = sb("trF", [64, P])[:, :]
        mu, root = smallf[:, 0:BLOCKS], smallf[:, 3 * CG:3 * CG + BLOCKS]

        s_const = sem("s_const")
        s_v = sem("s_v")
        s_w = sem("s_w")
        s_ld = sems("s_ld", 4)
        s_st = sems("s_st", 3)
        s_bc = sems("s_bc", 2)
        s_lde = sem("s_lde")
        s_xpad = sem("s_xpad")
        s_g = sems("s_g", 5)
        s_pt = sem("s_pt")
        s_pc = sem("s_pc")
        s_path = sem("s_path")
        s_path_in = sem("s_path_in")
        e_in = sems("e_in", EB)
        e_act = sems("e_act", EB)
        e_pool = sems("e_pool", EB)
        e_hot = sems("e_hot", EB)
        e_mm = sems("e_mm", EB)
        e_red = sems("e_red", EB)
        e_lnk = sem("e_lnk")
        e_add = sem("e_add")
        made = sem("made")
        stepped = sem("stepped")
        evacd = sem("evacd")
        stored = sems("stored", 2)
        a_in = [sems(f"a_in{j}_", 2) for j in range(2)]
        a_used = [sems(f"a_used{j}_", 2) for j in range(2)]
        d_red = sems("d_red", 2)
        staged = [sems(f"staged{r}_", 2) for r in range(3)]
        claimed = sem("claimed")
        gathered = [sems(f"gathered{r}_", 2) for r in range(3)]
        marked = [sems(f"marked{r}_", 2) for r in range(3)]
        gsum = [sems(f"gsum{r}_", 2) for r in range(3)]
        gred = [sems(f"gred{r}_", 2) for r in range(3)]
        s_add = sems("s_add", 3)
        round_done = sem("round_done")
        n_in = sem("n_in")
        n_t = sem("n_t")
        n_c = sem("n_c")
        n_v = sem("n_v")
        sp_turn = sem("sp_turn")
        n_turn = sem("n_turn")
        e_turn = sem("e_turn")
        n_eas = sems("n_eas", 2)
        s_ones = sem("s_ones")
        x1_st = sem("x1_st")
        y_st = sem("y_st")
        s_fin = sem("s_fin")
        s_root = sem("s_root")
        s_out = sem("s_out")

        block = ctx.enter_context(nc.Block())
        mark = {}

        NV, FEAT, NT, NC = (5, 18, 9), (0, 11, 1), (2, 4, 2), (1, 4, 2)
        vb = [1 + NITER * sum(NV[:r]) for r in range(4)]
        tb = [NITER * sum(NT[:r]) for r in range(4)]
        cb = [NITER * sum(NC[:r]) for r in range(4)]

        def load(engine, frm, n, top):
            _, v = nc.values_load_multi_w_load_instructions(
                path[0:1, bass.ds(frm, n)], engines=(engine,), min_val=0, max_val=top,
                skip_runtime_bounds_check_because="clamped to this range when the path was made")
            return v

        def flat(v):
            return v.rearrange("p b d -> p (b d)")

        @block.vector
        def _(dve):
            V = nc.vector
            count = [0]

            def step(ins, name=None):
                count[0] += 1
                ins.then_inc(s_v, 1)
                dve.wait_ge(s_v, count[0])
                if name:
                    mark[name] = count[0]

            for free in [*e_red, e_add, *d_red, *(y for z in gred for y in z), *s_add, n_v]:
                dve.sem_inc(free, 1)
            dve.wait_ge(s_const, CONSTS)
            for k in (1, 2, 3):
                step(V.memset(dtm[k][0:1, 0:k * P], -1000))
            dve.wait_ge(stored[0], 16)
            step(V.tensor_single_scalar(wtm, dtm[0], 2, op=ALU.arith_shift_right))
            for k in (1, 2, 3):
                dve.wait_ge(s_ld[k], 16 if k == 1 else 32)
                if k == 1:
                    dve.wait_ge(stored[1], 16)
                step(V.tensor_single_scalar(dtm[k], dtm[k], 2, op=ALU.arith_shift_right))
                step(V.tensor_tensor(dtf[k], dtm[k], wtm, ALU.is_equal))
            step(V.tensor_scalar(unc, dtm[0], float(D0), None, ALU.is_lt))
            for b, k in REGIONS:
                step(V.scalar_tensor_tensor(dtf[k], dtm[0], float(b * P), dtf[k], ALU.is_ge, ALU.mult))
                step(V.tensor_tensor(unc, unc, dtf[k], ALU.max))
            step(V.tensor_reduce(needt, unc.rearrange("p (t e) -> p t e", e=P), AX.X, ALU.max))
            step(V.tensor_copy(lastt, dtm[0].rearrange("p (t e) -> p t e", e=P)[:, :, P - 1]))
            step(V.scalar_tensor_tensor(dtf[1], unc, -FAR, dtm[0], ALU.mult, ALU.add))
            step(V.tensor_scalar(dtf[1], dtf[1], FAR, None, ALU.add), "left")
            dve.wait_ge(s_bc[0], 16)
            dve.wait_ge(s_bc[1], 16)
            step(V.tensor_copy(lastf_b, last_b))
            step(V.memset(junk, 1.0))
            step(V.tensor_tensor_scan(taken_b, junk, need_b, 0.0, ALU.mult, ALU.add))
            step(V.tensor_single_scalar(last_b, last_b, P.bit_length() - 1, op=ALU.arith_shift_right))
            step(V.scalar_tensor_tensor(leave_b, taken_b, -1.0, last_b, ALU.add, ALU.add))
            n_more = smallf[:, 15 * CG:15 * CG + 1]
            step(V.scalar_tensor_tensor(junk, leave_b, 1.0, need_b, ALU.add, ALU.mult))
            step(V.tensor_reduce(n_more, junk, AX.X, ALU.max))
            step(V.tensor_scalar(n_more, n_more, float(2 * G - 1 - BESIDE), 0.0, ALU.add, ALU.max))
            step(V.tensor_copy(gidx[:, 0, 0:1], n_more))
            step(V.tensor_single_scalar(gidx[:, 0, 0:1], gidx[:, 0, 0:1], (2 * G).bit_length() - 1,
                                        op=ALU.arith_shift_right))
            step(V.tensor_copy(n_more, gidx[:, 0, 0:1]))
            step(V.tensor_scalar(need_b, need_b, -FAR, FAR, ALU.mult, ALU.add))
            step(V.tensor_tensor(taken_b, leave_b, need_b, ALU.add))
            left_n, taken_n, blk_n, past_n, base_n = (small[:, k, 0:SG] for k in range(5))
            for g in range(SG):
                step(V.tensor_scalar(junk, leave_b, step_no[:, g:g + 1], 0.0, ALU.is_lt, ALU.add,
                                     accum_out=small[:, 0, g:g + 1]))
                step(V.tensor_scalar(junk2, taken_b, step_no[:, g:g + 1], 0.0, ALU.is_lt, ALU.add,
                                     accum_out=small[:, 1, g:g + 1]))
            step(V.tensor_scalar(blk_n, left_n, float(T - 1), None, ALU.min))
            step(V.tensor_copy(gidx[:, 0, 0:SG], blk_n))
            step(V.tensor_tensor(blk_n, step_no[:, :], taken_n, ALU.subtract))
            step(V.tensor_scalar(blk_n, blk_n, float(BLOCKS - 1), None, ALU.min))
            step(V.tensor_scalar(past_n, left_n, float(T), -FAR, ALU.is_ge, ALU.mult))
            step(V.scalar_tensor_tensor(base_n, blk_n, float(P), past_n, ALU.mult, ALU.add), "g_idx")
            for g in range(CG):
                step(V.tensor_scalar(junk, lastf_b, sc[:, 0, g:g + 1], 0.0, ALU.is_lt, ALU.add,
                                     accum_out=small[:, 5, g:g + 1]))
            step(V.tensor_scalar(small[:, 6, :], small[:, 5, :], float(T - 1), None, ALU.min))
            step(V.tensor_copy(gidx[:, 1, :], small[:, 6, :]), "c_tile")
            last_of = lastf_b.rearrange("p (g j) -> p g j", j=EG)[:, :, EG - 1]
            step(V.tensor_copy(junk[:, 0:GROUPS].bitcast(I32), last_of))
            step(V.tensor_single_scalar(junk[:, 0:GROUPS].bitcast(I32), junk[:, 0:GROUPS].bitcast(I32),
                                        P.bit_length() - 1, op=ALU.arith_shift_right))
            step(V.memset(junk2[:, 0:GROUPS], 1.0))
            step(V.tensor_tensor_scan(leave_e, junk2[:, 0:GROUPS], junk2[:, 0:GROUPS], -1.0, ALU.mult, ALU.add))
            step(V.tensor_tensor(leave_e, leave_e, junk[:, 0:GROUPS].bitcast(I32), ALU.add))
            e_left, e_grp, e_blk, e_base = (small[:, k, 0:ES] for k in range(7, 11))
            for g in range(ES):
                step(V.tensor_scalar(junk[:, 0:GROUPS], leave_e, step_no[:, g:g + 1], 0.0, ALU.is_lt, ALU.add,
                                     accum_out=small[:, 7, g:g + 1]))
            step(V.tensor_scalar(e_grp, e_left, float(GROUPS - 1), None, ALU.min))
            step(V.tensor_tensor(e_blk, step_no[:, 0:ES], e_left, ALU.subtract))
            step(V.tensor_scalar(e_blk, e_blk, float(BLOCKS - 1), None, ALU.min))
            step(V.tensor_scalar(e_base, e_left, float(GROUPS), -FAR, ALU.is_ge, ALU.mult))
            step(V.scalar_tensor_tensor(e_base, e_blk, float(P), e_base, ALU.mult, ALU.add))
            step(V.memset(regs, 0.0))
            for frm, to in ((blk_n, 0), (e_grp, 32), (e_blk, 40), (e_base, 48), (n_more, 56)):
                step(V.tensor_copy(regs[:, to:to + frm.shape[-1]], frm), "path")
            by_step = lambda t: t.rearrange("p (g e) -> p g e", e=P)
            over = lambda t, n: t.unsqueeze(2).to_broadcast([P, n, P])
            dve.wait_ge(s_g[0], 16 * SG)
            step(V.tensor_tensor(by_step(accf[:, 0:SPAD]), by_step(rows_gd), over(base_n, SG), ALU.subtract),
                 "rel_g")
            dve.wait_ge(s_g[1], 16 * SG)
            step(V.tensor_copy(easf[:, 0:SPAD], rows_gs), "src_g")
            dve.wait_ge(s_pc, 1 + 2 * BG)
            rel, tmp = accf[:, 0:CW], easf[:, 0:CW]
            dve.wait_ge(s_g[2], 16 * CG)
            step(V.tensor_tensor(by_step(rel), by_step(rows_ct), over(sc[:, 0, :], CG), ALU.is_lt))
            step(V.tensor_reduce(small[:, 0, :], by_step(rel), AX.X, ALU.add))
            step(V.scalar_tensor_tensor(small[:, 1, :], small[:, 6, :], float(P), small[:, 0, :],
                                        ALU.mult, ALU.add))
            step(V.tensor_tensor(small[:, 1, :], small[:, 1, :], sc[:, 1, :], ALU.add))
            step(V.tensor_scalar(small[:, 2, :], small[:, 1, :], float(E - P), None, ALU.min))
            step(V.tensor_copy(gidx[:, 2, :], small[:, 2, :]), "c_idx")
            step(V.tensor_tensor(small[:, 3, :], small[:, 1, :], small[:, 2, :], ALU.subtract))
            step(V.tensor_tensor(by_step(tmp), lanef[:, :].unsqueeze(1).to_broadcast([P, CG, P]),
                                 over(small[:, 3, :], CG), ALU.is_lt))
            dve.wait_ge(s_g[3], 16 * CG)
            step(V.tensor_tensor(by_step(rel), by_step(rows_cd), over(sc[:, 0, :], CG), ALU.subtract))
            step(V.scalar_tensor_tensor(tmp, rel, float(WD), tmp, ALU.is_ge, ALU.add))
            step(V.scalar_tensor_tensor(tmp, rel, 0.0, tmp, ALU.is_lt, ALU.add))
            step(V.scalar_tensor_tensor(rel, tmp, FAR, rel, ALU.mult, ALU.add))
            dve.wait_ge(s_g[4], 16 * CG)
            step(V.tensor_single_scalar(rows_cd, rows_cs, P.bit_length() - 1, op=ALU.arith_shift_right))
            step(V.scalar_tensor_tensor(rel, rows_cd, float(WD), rel, ALU.mult, ALU.add), "code_h")
            step(V.tensor_single_scalar(rows_cs, rows_cs, P - 1, op=ALU.bitwise_and))
            step(V.tensor_copy(tmp, rows_cs), "code_l")
            dve.wait_ge(s_lde, 16)
            step(V.tensor_copy(dst_rows, dst_rows.bitcast(I32)), "dst_e")
            dve.wait_ge(s_pc, 1 + 2 * BG + 2 * BC + BE)
            step(V.memset(eas[:, :, :], 0.0))
            for v in parts4:
                step(V.memset(v[:, :, :, D:F1], 0.0))
                step(V.memset(v[:, :, 0, D:F1], 1.0), "ones_e")
            step(V.memset(acc[:, :, :], 0.0))
            dve.wait_ge(s_w, 16 * LOADS)
            for c in range(2):
                step(V.tensor_tensor(bme[:, c, 0, :], bme[:, c, 0, :], bme[:, c, 1, :], ALU.add))
            dve.wait_ge(s_path_in, 32)

            def e_mark(h, it, grp, s, n):
                dve.wait_ge(e_mm[h], it + 1)
                V.tensor_scalar(rel_e[:, h, :], flat(dst_e[:, bass.ds(grp, 1), :]), base_e[:, bass.ds(s, 1)],
                                None, ALU.subtract).then_inc(e_lnk, 1)
                dve.wait_ge(e_lnk, n)
                V.tensor_tensor(hot_e[:, h, :, :], rel_e[:, h, :].unsqueeze(2).to_broadcast([P, EG, P]),
                                lane16[:, 0:P].unsqueeze(1).to_broadcast([P, EG, P]), ALU.is_equal)\
                    .then_inc(e_hot[h], 1)

            first = load(ENG.DVE, SPAD, 1, GROUPS - 1)
            dve.wait_ge(e_mm[0], 1)
            V.tensor_scalar(rel_e[:, 0, :], flat(dst_e[:, bass.ds(first[0], 1), :]), base_e[:, 0:1], None,
                            ALU.subtract).then_inc(e_lnk, 1)
            dve.wait_ge(e_lnk, 1)
            V.tensor_tensor(hot_e[:, 0, :, :], rel_e[:, 0, :].unsqueeze(2).to_broadcast([P, EG, P]),
                            lane16[:, 0:P].unsqueeze(1).to_broadcast([P, EG, P]), ALU.is_equal)\
                .then_inc(e_hot[0], 1)
            with dve.Fori(0, ESTEPS // EB) as i:
                grp = load(ENG.DVE, i * EB + (SPAD + 1), EB, GROUPS - 1)
                bs = load(ENG.DVE, i * EB + (SPAD + ES * P), EB, BLOCKS - 1)
                for h in range(EB):
                    e_mark((h + 1) % EB, i + (h + 1) // EB, grp[h], i * EB + (h + 1), i * EB + (h + 2))
                    dve.wait_ge(e_mm[h], i + 2)
                    V.tensor_reduce(part_e[:, h, :], ps[:, h, 0:3 * F1].rearrange("p (c d) -> p d c", d=F1),
                                    AX.X, ALU.add).then_inc(e_red[h], 1)
                    dve.wait_ge(e_red[h], i + 2)
                    dve.wait_ge(e_add, i * EB + (h + 1))
                    to = flat(eas[:, bass.ds(bs[h], 1), :])
                    V.tensor_tensor(to, to, part_e[:, h, :], ALU.add).then_inc(e_add, 1)
            dve.wait_ge(e_add, ESTEPS + 1)
            step(V.tensor_scalar(rdeg[:, :], eas[:, :, D], 1.0, None, ALU.max))
            step(V.reciprocal(rdeg[:, :], rdeg[:, :]), "rdeg")

            for b0, blocks, K, s0 in REG:
                with dve.Fori(0, blocks // 2) as i:
                    for j in range(2):
                        for m in range(WPB * K // 8):
                            base = j * WPB * K + 8 * m + s0
                            dve.wait_ge(stepped, i * (2 * WPB * K) + (base + 1))
                            for e in range(8):
                                n, s = m % 2 * 8 + e, bass.ds(i * (2 * WPB * K) + (base + e), 1)
                                V.tensor_scalar(hot_c[:, n, 0:WIN], lane16[:, :], code_h[:, s], None, ALU.is_equal)
                                last = V.tensor_scalar(hot_c[:, n, WIN:WIN + P], lane16[:, 0:P], code_l[:, s],
                                                       None, ALU.is_equal)
                            last.then_inc(made, 1)
            dve.wait_ge(stepped, CSTEPS + 9)

            for r in range(3):
                if r == 0:
                    for j in range(2):
                        dve.wait_ge(stored[j], 16 * (ITERS + 1))
                V.memset(xT[D:F1, :], 1.0).then_inc(s_ones, 1)
                with dve.Fori(0, NITER) as i:
                    n = [0]

                    def vstep(ins):
                        n[0] += 1
                        ins.then_inc(n_v, 1)
                        dve.wait_ge(n_v, i * NV[r] + (n[0] + vb[r]))

                    blk = bass.ds(i * NB, NB)
                    bc = lambda t: t.unsqueeze(2).to_broadcast([P, NB, D])
                    bank = lambda k: ps[:, k, 0:NB * D].rearrange("p (b d) -> p b d", d=D)
                    if r:
                        dve.wait_ge(n_in, i * 16 + (16 + 16 * NITER * r))
                    if r == 1:
                        vstep(V.tensor_tensor(t2, acc[:, blk, :], bc(rdeg[:, blk]), ALU.mult))
                        dve.wait_ge(n_t, i * NT[r] + (2 + tb[r]))
                        vstep(V.tensor_tensor(t2, t2, bank(2), ALU.add))
                        vstep(V.scalar_tensor_tensor(t2, t2, 0.0, bank(3), ALU.max, ALU.add))
                        vstep(V.tensor_tensor(t2, t2, nrow, ALU.add))
                        vstep(V.tensor_reduce(mean[:, :], t2, AX.X, ALU.add))
                        vstep(V.tensor_scalar(mean[:, :], mean[:, :], 1.0 / D, None, ALU.mult))
                        vstep(V.tensor_tensor(t2, t2, bc(mean[:, :]), ALU.subtract))
                        vstep(V.tensor_tensor(feat, t2, t2, ALU.mult))
                        vstep(V.tensor_reduce(mean[:, :], feat, AX.X, ALU.add))
                        dve.wait_ge(n_c, i * NC[r] + (2 + cb[r]))
                        vstep(V.reciprocal(sdev[:, :], sdev[:, :]))
                        vstep(V.tensor_tensor(feat, t2, bc(sdev[:, :]), ALU.mult))
                    elif r == 2:
                        vstep(V.tensor_scalar(feat, acc[:, blk, :], 0.0, None, ALU.max))
                    assert n[0] == FEAT[r]
                    dve.wait_ge(n_t, i * NT[r] + (NT[r] + tb[r]))
                    y = [yparts[:, blk, c, :] for c in range(3)]
                    vstep(V.tensor_copy(y[0], bank(2)))
                    vstep(V.tensor_tensor(t2, bank(2), y[0], ALU.subtract))
                    vstep(V.tensor_copy(y[1], t2))
                    vstep(V.tensor_tensor(t2, t2, y[1], ALU.subtract))
                    vstep(V.tensor_copy(y[2], t2))
                    if r:
                        vstep(V.tensor_tensor(t2, bme[:, r - 1, 0, :].unsqueeze(1).to_broadcast([P, NB, D]),
                                              eas[:, blk, D:F1].to_broadcast([P, NB, D]), ALU.mult))
                        vstep(V.tensor_tensor(acc[:, blk, :], t2, bank(3), ALU.add))
                        if r == 2:
                            vstep(V.tensor_tensor(acc[:, blk, :], acc[:, blk, :], nrow, ALU.add))
                    assert n[0] == NV[r]

                def g_mark(it, j):
                    dve.wait_ge(gsum[r][j], it + 1)
                    V.tensor_tensor(hot_g[:, j * G:(j + 1) * G, :],
                                    code_g[:, bass.ds((it * 2 + j) * G, G)].unsqueeze(2).to_broadcast([P, G, P]),
                                    lane16[:, 0:P].unsqueeze(1).to_broadcast([P, G, P]), ALU.is_equal)\
                        .then_inc(marked[r][j], 1)

                def g_add(it, j, before):
                    bs = load(ENG.DVE, (it * 2 + j) * G, G, BLOCKS - 1)
                    dve.wait_ge(gsum[r][j], it + 2)
                    for k in range(0, G, 2):
                        V.tensor_reduce(part_g[:, k:k + 2, :],
                                        ps[:, 2 + k // 2, 0:6 * D].rearrange("p (a c d) -> p a d c", a=2, c=3),
                                        AX.X, ALU.add).then_inc(gred[r][j], 1)
                    dve.wait_ge(gred[r][j], it * (G // 2) + (G // 2 + 1))
                    for k in range(G):
                        to = flat(acc[:, bass.ds(bs[k], 1), :])
                        V.tensor_tensor(to, to, part_g[:, k, :], ALU.add).then_inc(s_add[r], 1)
                        dve.wait_ge(s_add[r], before + (k + 1))

                with dve.Fori(0, ITERS) as i:
                    for j in range(2):
                        g_mark(i, j)
                        dve.wait_ge(a_used[j][1], i + (2 + r * ITERS))
                        V.tensor_reduce(part_d[:, j, :], ps[:, j, 0:3 * D].rearrange("p (c d) -> p d c", c=3),
                                        AX.X, ALU.add).then_inc(d_red[j], 1)
                        dve.wait_ge(d_red[j], i + (2 + r * ITERS))
                        before = i * (2 * (G + 1)) + (1 + j * (G + 1))
                        to = flat(acc[:, bass.ds(i * 2 + (B0 + j), 1), :])
                        V.tensor_tensor(to, to, part_d[:, j, :], ALU.add).then_inc(s_add[r], 1)
                        dve.wait_ge(s_add[r], before + 1)
                        g_add(i, j, before + 1)
                more = load(ENG.DVE, PATH - P, 1, MORE)[0]
                with dve.If(more > 0):
                    with dve.Fori(0, more) as i:
                        for j in range(2):
                            g_mark(i + ITERS, j)
                            g_add(i + ITERS, j, i * (2 * G) + (1 + DB * (G + 1) + j * G))
                dve.sem_inc(round_done, 1)

            fin = [0]

            def last_step(ins):
                fin[0] += 1
                ins.then_inc(s_fin, 1)
                dve.wait_ge(s_fin, fin[0])

            squares = union[:, 0:BLOCKS * D].rearrange("p (b d) -> p b d", d=D)
            wide = lambda t: t.unsqueeze(2).to_broadcast([P, BLOCKS, D])
            last_step(V.tensor_reduce(mu, acc[:, :, :], AX.X, ALU.add))
            last_step(V.tensor_scalar(mu, mu, 1.0 / D, None, ALU.mult))
            last_step(V.tensor_tensor(acc[:, :, :], acc[:, :, :], wide(mu), ALU.subtract))
            last_step(V.tensor_tensor(squares, acc[:, :, :], acc[:, :, :], ALU.mult))
            last_step(V.tensor_reduce(mu, squares, AX.X, ALU.add))
            dve.wait_ge(s_root, 1)
            last_step(V.reciprocal(root, root))
            last_step(V.tensor_tensor(acc[:, :, :], acc[:, :, :], wide(root), ALU.mult))

        jobs = [(mark["path"], [(regs, 64, P, trT)])]
        for frm, name, to, cols in ((accf, "rel_g", code_g, SG), (easf, "src_g", src_g, SG),
                                    (accf, "code_h", code_h, CG), (easf, "code_l", code_l, CG)):
            for g0 in range(0, cols, 4):
                jobs.append((mark[name], [(frm[:, g * P:(g + 1) * P], P, P, to[:, g * P:(g + 1) * P])
                                          for g in range(g0, min(g0 + 4, cols))]))
        e_src = dst_rows.rearrange("p (a q j) -> p a j q", a=TC // EG, j=EG)
        e_dst = dst_e.rearrange("p (q a) j -> p a j q", a=TC // EG)
        pieces = [(e_src[:, a, j, :], P, TP, e_dst[:, a, j, :]) for a in range(TC // EG) for j in range(EG)]
        for g0 in range(0, len(pieces), 4):
            jobs.append((mark["dst_e"], pieces[g0:g0 + 4]))
        assert len(jobs) == 1 + 2 * BG + 2 * BC + BE

        @block.tensor
        def _(pe):
            for free in [*e_mm, *(y for z in a_used for y in z), *(y for z in gsum for y in z)]:
                pe.sem_inc(free, 1)
            pe.sem_inc(stepped, 9)
            pe.wait_ge(s_const, CONSTS)
            for n, (ready, items) in enumerate(jobs):
                pe.wait_ge(s_v, ready)
                if n >= 4:
                    pe.wait_ge(s_pc, n - 3)
                for c, (frm, m, k, _) in enumerate(items):
                    last = pe.transpose(ps[0:m, n % 4, c * P:c * P + k], frm, ident[0:k, 0:k])
                last.then_inc(s_pt, 1)
            pe.wait_ge(s_pc, len(jobs))
            with pe.Fori(0, ESTEPS // EB) as i:
                for h in range(EB):
                    pe.wait_ge(e_pool[h], i * 2 + 4)
                    pe.wait_ge(e_hot[h], i + 1)
                    pe.wait_ge(e_red[h], i + 1)
                    for j in range(EG):
                        last = nc.tensor.matmul(ps[:, h, 0:3 * F1], hot_e[:, h, j, :], parts3[h][:, j, :],
                                                start=j == 0, stop=j == EG - 1)
                    last.then_inc(e_mm[h], 1)
            for b0, blocks, K, s0 in REG:
                with pe.Fori(0, blocks // 2) as i:
                    for j in range(2):
                        for q in range(WPB * K):
                            w, c = q // K, q % K
                            if q % 8 == 0:
                                pe.wait_ge(made, i * (2 * WPB * K // 8) + (j * WPB * K // 8 + q // 8 + s0 // 8 + 1))
                            if c == 0 and w % 4 == 0:
                                pe.wait_ge(evacd, i * (2 * WPB) + ((b0 + j) * WPB + w + 1))
                            n = q % 16
                            nc.tensor.matmul(ps[:, w % 8, 0:WIN], hot_c[:, n, WIN:WIN + P], hot_c[:, n, 0:WIN],
                                             start=c == 0, stop=c == K - 1).then_inc(stepped, 1)
            for r in range(3):
                if r == 0:
                    pe.wait_ge(evacd, DB * WPB + 5)
                else:
                    pe.wait_ge(round_done, r)
                pe.wait_ge(s_ones, r + 1)
                pe.wait_ge(s_w, 16 * LOADS)
                with pe.Fori(0, NITER) as i:
                    def turn(rows, first_bank, last_inc=True):
                        for b in range(NB):
                            k = first_bank + b // 4
                            last = pe.transpose(ps[0:D, k, b % 4 * P:(b % 4 + 1) * P], rows(b), ident[:, :])
                        return last

                    if r < 2:
                        pe.wait_ge(n_in, i * 16 + (16 + 16 * NITER * r))
                        pe.sem_inc(n_turn, 1)
                        turn(lambda b: nrow[:, b, :], 0).then_inc(n_t, 1)
                        pe.wait_ge(n_c, i * NC[r] + (1 + cb[r]))
                    if r == 1:
                        for b in range(NB):
                            for c in range(2):
                                last = nc.tensor.matmul(ps[:, 2 + c, b * D:(b + 1) * D], xT[:, b * P:(b + 1) * P],
                                                        w_in[:, c, :], start=True, stop=True)
                        last.then_inc(n_t, 1)
                    if r:
                        pe.wait_ge(n_v, i * NV[r] + (FEAT[r] + vb[r]))
                        pe.wait_ge(n_eas[r - 1], i + 1)
                        pe.sem_inc(n_turn, 1)
                        turn(lambda b: feat[:, b, :], 0)
                        turn(lambda b: ecopy[:, b, :], 4).then_inc(n_t, 1)
                        pe.wait_ge(n_c, i * NC[r] + (NC[r] + cb[r]))
                    for b in range(NB):
                        last = nc.tensor.matmul(ps[:, 2, b * D:(b + 1) * D], xT[0:D, b * P:(b + 1) * P],
                                                w_y[:, r, :], start=True, stop=True)
                    if r:
                        for b in range(NB):
                            nc.tensor.matmul(ps[:, 3, b * D:(b + 1) * D], xT[:, b * P:(b + 1) * P],
                                             w_s[:, r - 1, :], start=True, stop=False)
                            last = nc.tensor.matmul(ps[:, 3, b * D:(b + 1) * D], eT[:, b * P:(b + 1) * P],
                                                    w_e[:, r - 1, :], start=False, stop=True)
                    last.then_inc(n_t, 1)
                pe.wait_ge(n_v, vb[r + 1])

                def g_multiply(it, j, other):
                    pe.wait_ge(marked[r][j], it + 1)
                    pe.wait_ge(gathered[r][j], (it + 1) * (16 * G))
                    pe.wait_ge(gred[r][1 - j], other)
                    for k in range(G):
                        s = j * G + k
                        last = nc.tensor.matmul(ps[:, 2 + k // 2, k % 2 * 3 * D:(k % 2 + 1) * 3 * D],
                                                hot_g[:, s, :], msg[:, s, :], start=True, stop=True)
                    last.then_inc(gsum[r][j], 1)

                with pe.Fori(0, ITERS) as i:
                    for j in range(2):
                        pe.wait_ge(d_red[j], i + (1 + r * ITERS))
                        for u in range(2):
                            pe.wait_ge(a_in[j][u], i * 16 + 16 * (1 + r * ITERS))
                            for h in range(HALF):
                                hi = u * HALF + h
                                last = nc.tensor.matmul(ps[:, j, 0:3 * D], abuf[:, j, hi * P:(hi + 1) * P],
                                                        ycols[:, hi, :], start=hi == 0, stop=hi == HIS - 1)
                            last.then_inc(a_used[j][u], 1)
                        g_multiply(i, j, (i + j) * (G // 2) + 1)
                more = load(ENG.PE, PATH - P, 1, MORE)[0]
                with pe.If(more > 0):
                    with pe.Fori(0, more) as i:
                        for j in range(2):
                            g_multiply(i + ITERS, j, (i + (ITERS + j)) * (G // 2) + 1)

        @block.gpsimd
        def _(pool):
            for free in e_pool:
                pool.sem_inc(free, 2)
            pool.memset(zpad[:, :], 0.0).then_inc(s_const, 1)
            pool.memset(ident[:, :], 0.0).then_inc(s_const, 1)
            pool.iota(step_no[:, :], [[P, SG]], base=0, channel_multiplier=1,
                      allow_small_or_imprecise_dtypes=True).then_inc(s_const, 1)
            pool.iota(lane16[:, :], [[1, WIN]], base=0, channel_multiplier=0,
                      allow_small_or_imprecise_dtypes=True).then_inc(s_const, 1)
            pool.iota(lanef[:, :], [[1, P]], base=0, channel_multiplier=0,
                      allow_small_or_imprecise_dtypes=True).then_inc(s_const, 1)
            pool.memset(epst[:, :], EPS).then_inc(s_const, 1)
            pool.wait_ge(s_const, 2)
            pool.affine_select(out=ident[:, :], in_=ident[:, :], compare_op=ALU.not_equal, fill=1.0,
                               base=0, pattern=[[-1, P]], channel_multiplier=1).then_inc(s_const, 1)
            tiles = lambda a: a.rearrange("(t e) -> t e", e=P)
            single = lambda a: a.rearrange("(e o) -> e o", o=1)

            def fetch(rows, table, which, cols, done):
                for g in range(cols):
                    pool.indirect_dma_start(rows[:, g * P:(g + 1) * P], None, table, bass.IndirectOffsetOnAxis(
                        ap=gidx[:, which, g:g + 1], axis=0)).then_inc(done, 16)

            pool.wait_ge(s_v, mark["g_idx"])
            pool.wait_ge(s_st[0], 16)
            fetch(rows_gd, left_dram, 0, SG, s_g[0])
            fetch(rows_gs, tiles(src), 0, SG, s_g[1])
            pool.wait_ge(s_v, mark["c_tile"])
            fetch(rows_ct, tiles(dst), 1, CG, s_g[2])
            pool.wait_ge(s_v, mark["c_idx"])
            fetch(rows_cd, single(dst), 2, CG, s_g[3])
            fetch(rows_cs, single(src), 2, CG, s_g[4])
            with pool.Fori(0, ESTEPS // EB) as i:
                def remainder(h):
                    pool.wait_ge(e_act[h], i * 2 + 1)
                    nc.gpsimd.tensor_tensor(rests[:, h, :, :], feats[:, h, :, :], parts4[h][:, :, 0, 0:D],
                                            ALU.subtract).then_inc(e_pool[h], 1)

                def third(h):
                    pool.wait_ge(e_act[h], i * 2 + 2)
                    nc.gpsimd.tensor_tensor(parts4[h][:, :, 2, 0:D], rests[:, h, :, :], parts4[h][:, :, 1, 0:D],
                                            ALU.subtract).then_inc(e_pool[h], 1)

                remainder(0)
                for h in range(1, EB):
                    remainder(h)
                    third(h - 1)
                third(EB - 1)
            for r in range(3):
                pool.wait_ge(y_st, 16 * NITER * (r + 1))

                def g_fetch(it, j):
                    pool.wait_ge(staged[r][j], it + 1)
                    pool.sem_inc(claimed, 1)
                    for k in range(G):
                        s = j * G + k
                        pool.indirect_dma_start(msg[:, s, :], None, y_tab, bass.IndirectOffsetOnAxis(
                            ap=idx[:, s:s + 1], axis=0)).then_inc(gathered[r][j], 16)

                with pool.Fori(0, ITERS) as i:
                    for j in range(2):
                        g_fetch(i, j)
                more = load(ENG.Pool, PATH - P, 1, MORE)[0]
                with pool.If(more > 0):
                    with pool.Fori(0, more) as i:
                        for j in range(2):
                            g_fetch(i + ITERS, j)

        @block.scalar
        def _(act):
            A = nc.scalar
            act.sem_inc(evacd, 5)
            for n, (_, items) in enumerate(jobs):
                act.wait_ge(s_pt, n + 1)
                if n == 0:
                    A.activation(trT, ps[0:64, 0, 0:P], ACT.Copy)
                    last = A.activation(trF, ps[0:64, 0, 0:P], ACT.Copy)
                else:
                    for c, (_, m, k, to) in enumerate(items):
                        last = A.activation(to, ps[0:m, n % 4, c * P:c * P + k], ACT.Copy)
                last.then_inc(s_pc, 1)
            act.wait_ge(s_v, mark["ones_e"])
            with act.Fori(0, ESTEPS // EB) as i:
                def part1(h):
                    act.wait_ge(e_mm[h], i + 1)
                    act.wait_ge(e_in[h], i * 16 + 16)
                    act.sem_inc(e_turn, 1)
                    A.activation(parts4[h][:, :, 0, 0:D], feats[:, h, :, :], ACT.Copy).then_inc(e_act[h], 1)

                def part2(h):
                    act.wait_ge(e_pool[h], i * 2 + 3)
                    A.activation(parts4[h][:, :, 1, 0:D], rests[:, h, :, :], ACT.Copy).then_inc(e_act[h], 1)

                part1(0)
                for h in range(1, EB):
                    part1(h)
                    part2(h - 1)
                part2(EB - 1)
            for b0, blocks, K, s0 in REG:
                with act.Fori(0, blocks // 2) as i:
                    for j in range(2):
                        act.wait_ge(stored[j], i * 16 + 16 * (b0 // 2 + 1))
                        act.sem_inc(e_turn, 1)
                        for w in range(WPB):
                            act.wait_ge(stepped, i * (2 * WPB * K) + ((j * WPB + w + 1) * K + s0 + 9))
                            A.activation(abuf[:, j, :].rearrange("p (h d) -> p h d", d=P)[:, :, w * WD:(w + 1) * WD],
                                         ps[:, w % 8, 0:WIN].rearrange("p (h d) -> p h d", d=WD), ACT.Copy)\
                                .then_inc(evacd, 1)
            for r in range(3):
                if r:
                    act.wait_ge(round_done, r)
                with act.Fori(0, NITER) as i:
                    def turned(to, k):
                        return A.activation(to, ps[0:D, k:k + 2, :].rearrange("p k c -> p (k c)")[:, 0:NB * P], ACT.Copy)

                    if r:
                        act.wait_ge(n_v, i * NV[r] + vb[r])
                        A.activation(ecopy, eas[:, bass.ds(i * NB, NB), 0:D], ACT.Copy).then_inc(n_eas[r - 1], 1)
                    if r < 2:
                        act.wait_ge(n_t, i * NT[r] + (1 + tb[r]))
                        turned(xT[0:D, :], 0).then_inc(n_c, 1)
                    if r == 1:
                        act.wait_ge(n_v, i * NV[r] + (9 + vb[r]))
                        A.activation(sdev[:, :], mean[:, :], ACT.Sqrt, bias=epst[:, :], scale=1.0 / D).then_inc(n_c, 1)
                    if r:
                        act.wait_ge(n_t, i * NT[r] + (NT[r] - 1 + tb[r]))
                        turned(xT[0:D, :], 0).then_inc(n_c, 1)
                        turned(eT, 4).then_inc(n_c, 1)

                def g_stage(it, j):
                    act.wait_ge(gsum[r][j], it + 1)
                    A.activation(idx[:, j * G:(j + 1) * G], src_g[:, bass.ds((it * 2 + j) * G, G)], ACT.Copy)\
                        .then_inc(staged[r][j], 1)

                with act.Fori(0, ITERS) as i:
                    for j in range(2):
                        g_stage(i, j)
                more = load(ENG.Activation, PATH - P, 1, MORE)[0]
                with act.If(more > 0):
                    with act.Fori(0, more) as i:
                        for j in range(2):
                            g_stage(i + ITERS, j)
            act.wait_ge(s_fin, 5)
            A.activation(root, mu, ACT.Sqrt, bias=epst[:, :], scale=1.0 / D).then_inc(s_root, 1)

        @block.sync
        def _(sp):
            sp.dma_start(dtm[0], dst.rearrange("(p c) -> p c", p=TP)).then_inc(stored[0], 16)
            for k in (1, 2, 3):
                a, b = TW - k * P, TW - k * P + (TP - 1) * TW
                sp.dma_start(dtm[k][1:TP, :], dst[a:b].rearrange("(p c) -> p c", p=TP - 1))\
                  .then_inc(stored[1] if k == 1 else s_ld[k], 16)
                sp.dma_start(dtm[k][0:1, k * P:TW], dst[0:a].rearrange("(p c) -> p c", p=1)).then_inc(s_ld[k], 16)
            row = lambda a: a.rearrange("(a n) -> a n", a=1)
            loads = [(sc[:, :, :], step_c), (w_in[0:D, 0, :], W_fc[0:D, :]), (w_in[0:D, 1, :], W_res),
                     (w_in[D:F1, 0, :], row(b_fc)), (w_in[D:F1, 1, :], row(b_res)), (w_y[:, 0, :], W_fc[D:2 * D, :])]
            for c, (wm, we, s_, bm, be, bs) in enumerate(((Wm1, We1, Ws1, bm1, be1, bs1),
                                                          (Wm2, We2, Ws2, bm2, be2, bs2))):
                loads += [(w_y[:, 1 + c, :], wm), (w_e[:, c, :], we), (w_s[0:D, c, :], s_),
                          (w_s[D:F1, c, :], row(bs)), (bme[:, c, 0, :], row(bm).to_broadcast([P, D])),
                          (bme[:, c, 1, :], row(be).to_broadcast([P, D]))]
            assert len(loads) == LOADS
            for to, frm in loads:
                sp.dma_start(to, frm).then_inc(s_w, 16)
            sp.dma_start(x_pad[0:N, :], x).then_inc(s_xpad, 16)
            sp.wait_ge(s_const, 1)
            sp.dma_start(x_pad[N:NPAD, :], zpad[:, :]).then_inc(s_xpad, 16)
            sp.wait_ge(s_v, mark["left"])
            sp.dma_start(last_dram.rearrange("(p t) -> p t", p=TP), lastt).then_inc(s_st[1], 16)
            sp.dma_start(need_dram.rearrange("(p t) -> p t", p=TP), needt).then_inc(s_st[2], 16)
            sp.dma_start(left_dram.rearrange("(p t) e -> p (t e)", p=TP), dtf[1]).then_inc(s_st[0], 16)
            for k in range(3):
                sp.wait_ge(s_st[k], 16)
            sp.dma_start(last_b, row(last_dram).to_broadcast([P, T])).then_inc(s_bc[0], 16)
            sp.dma_start(need_b, row(need_dram).to_broadcast([P, T])).then_inc(s_bc[1], 16)
            sp.wait_ge(s_pc, 1)
            for frm, to, cols in ((0, 0, SG), (32, SPAD, ES), (40, SPAD + ES * P, ES), (56, PATH - P, 1)):
                sp.dma_start(path_dram[to:to + cols * P].rearrange("(g p) -> g p", p=P), trT[frm:frm + cols, :])\
                  .then_inc(s_path, 16)
            sp.dma_start(base_dram.rearrange("(g p) -> g p", p=P), trF[48:48 + ES, :]).then_inc(s_path, 16)
            sp.wait_ge(s_path, 80)
            sp.dma_start(path[:, :], row(path_dram)).then_inc(s_path_in, 16)
            sp.dma_start(base_e[:, :], row(base_dram).to_broadcast([P, ES * P])).then_inc(s_path_in, 16)
            sp.wait_ge(s_v, mark["code_l"])
            sp.dma_start(dst_rows.bitcast(I32), dst.rearrange("(p c) -> p c", p=TP)).then_inc(s_lde, 16)
            sp.wait_ge(s_path_in, 32)
            sp.wait_ge(s_pc, len(jobs))
            ea = edge_attr.rearrange("(g p j) d -> g p (j d)", p=P, j=EG)
            with sp.Fori(0, ESTEPS // EB) as i:
                grp = load(ENG.SP, i * EB + SPAD, EB, GROUPS - 1)
                for h in range(EB):
                    sp.wait_ge(e_pool[h], i * 2 + 1)
                    sp.sem_inc(sp_turn, 1)
                    sp.dma_start(feats[:, h, :, :].rearrange("p j d -> p (j d)"), ea[bass.ds(grp[h], 1), :, :].rearrange("g p c -> (g p) c"))\
                      .then_inc(e_in[h], 16)
            for b0, blocks, K, s0 in REG:
                with sp.Fori(0, blocks // 2) as i:
                    for j in range(2):
                        sp.wait_ge(evacd, i * (2 * WPB) + ((b0 + j + 1) * WPB + 5))
                        sp.sem_inc(sp_turn, 1)
                        sp.dma_start(a_dram[j][bass.ds(i + b0 // 2, 1), :, :, :]
                                     .rearrange("b u p c -> p (b u) c"),
                                     abuf[:, j, :].rearrange("p (u c) -> p u c", u=2)).then_inc(stored[j], 16)
            for j in range(2):
                sp.wait_ge(stored[j], 16 * (ITERS + 1))
            sp.wait_ge(s_xpad, 32)
            for r, table in enumerate((x_pad, x_pad, x1_tab)):
                if r:
                    sp.wait_ge(round_done, r)
                rows = table.rearrange("(b p) d -> p b d", p=P)
                with sp.Fori(0, NITER) as i:
                    sp.wait_ge(n_v, i * NV[r] + vb[r])
                    sp.sem_inc(sp_turn, 1)
                    sp.dma_start(nrow, rows[:, bass.ds(i * NB, NB), :]).then_inc(n_in, 16)
                    if r == 1:
                        sp.wait_ge(n_v, i * NV[r] + (FEAT[r] + vb[r]))
                        sp.sem_inc(sp_turn, 1)
                        sp.dma_start(x1_tab.rearrange("(b p) d -> p b d", p=P)[:, bass.ds(i * NB, NB), :], feat)\
                          .then_inc(x1_st, 16)
                        sp.wait_ge(x1_st, i * 16 + 16)
                        sp.sem_inc(sp_turn, 1)
                    sp.wait_ge(n_v, i * NV[r] + (FEAT[r] + 5 + vb[r]))
                    sp.sem_inc(sp_turn, 1)
                    sp.dma_start(y_tab.rearrange("(b p) c -> p b c", p=P)[:, bass.ds(i * NB, NB), :],
                                 ycols[:, bass.ds(i * NB, NB), :]).then_inc(y_st, 16)
                sp.wait_ge(n_v, vb[r + 1])
                with sp.Fori(0, ITERS) as i:
                    for j in range(2):
                        for u in range(2):
                            sp.wait_ge(a_used[j][u], i + (1 + r * ITERS))
                            sp.sem_inc(sp_turn, 1)
                            sp.dma_start(abuf[:, j, u * HALF * P:(u + 1) * HALF * P],
                                         a_dram[j][bass.ds(i, 1), u, :, :].rearrange("b p c -> p (b c)"))\
                              .then_inc(a_in[j][u], 16)
            sp.wait_ge(y_st, 16 * NITER * 3)
            sp.wait_ge(s_fin, 7)
            sp.dma_start(out[0:FULL * P, :].rearrange("(b p) d -> p b d", p=P), acc[:, 0:FULL, :]).then_inc(s_out, 16)
            sp.dma_start(out[FULL * P:N, :], acc[0:REST, FULL, :]).then_inc(s_out, 16)
            sp.wait_ge(s_out, 32)


CONSTS = 7
LOADS = 18


_INS = ['x', 'src', 'dst', 'edge_attr_64', 'L0_gnn_W_fc', 'L0_gnn_b_fc', 'L0_gnn_W_res', 'L0_gnn_b_res',
        'L1_gnn_Wm1', 'L1_gnn_bm1', 'L1_gnn_We1', 'L1_gnn_be1', 'L1_gnn_Ws1', 'L1_gnn_bs1',
        'L1_gnn_Wm2', 'L1_gnn_bm2', 'L1_gnn_We2', 'L1_gnn_be2', 'L1_gnn_Ws2', 'L1_gnn_bs2']
_OUTS = [((12500, 64), 'float32')]


def kernel(**inputs):
    import numpy as _np
    import concourse.bacc as _bacc
    from concourse import mybir as _mybir
    from concourse.bass_utils import run_bass_kernel_spmd as _run

    nc = _bacc.Bacc("TRN2", target_bir_lowering=False, num_devices=1)
    arrays, args = {"in_step_constants": step_constants()}, []
    for name in _INS:
        arrays[f"in_{name}_dram"] = _np.ascontiguousarray(inputs[name])
    for name, a in arrays.items():
        args.append(nc.dram_tensor(name, a.shape, _mybir.dt.from_np(a.dtype), kind="ExternalInput").ap())
    for i, (shape, dtype) in enumerate(_OUTS):
        dt = _mybir.dt.from_np(_np.dtype(dtype))
        args.append(nc.dram_tensor(f"out_{i}_dram", shape, dt, kind="ExternalOutput").ap())
    gnn_program(nc, *args)
    r = _run(nc, [arrays], core_ids=[0])
    return r.results[0]["out_0_dram"]
```

```python
from contextlib import ExitStack

import concourse.bass as bass
from concourse import mybir

F32 = mybir.dt.float32
F16 = mybir.dt.float16
BF16 = mybir.dt.bfloat16
I32 = mybir.dt.int32
I16 = mybir.dt.int16
ALU = mybir.AluOpType
ACT = mybir.ActivationFunctionType
ENG = mybir.EngineType
AX = mybir.AxisListType

P = 128
EPS = 1e-5
WD = 4
N_NODES, N_EDGES = 12500, 400000
BLOCKS = -(-N_NODES // P)
REGIONS = ((4, 3), (6, 2), (28, 1))
WPB = P // WD


def regions():
    found, step = [], 0
    for n, (b, k) in enumerate(REGIONS):
        end = REGIONS[n + 1][0] if n + 1 < len(REGIONS) else BLOCKS
        found.append((b - REGIONS[0][0], end - b, k, step))
        step += (end - b) * WPB * k
    return found, step


def step_constants():
    import numpy as np
    found, steps = regions()
    cols = -(-steps // P)
    first = np.full(cols * P, 1.0e6, np.float32)
    offset = np.zeros(cols * P, np.float32)
    for b0, blocks, k, s0 in found:
        q = np.arange(blocks * WPB * k)
        first[s0 + q] = (REGIONS[0][0] + b0) * P + q // k * WD
        offset[s0 + q] = q % k * P
    return np.ascontiguousarray(np.stack([first.reshape(cols, P).T, offset.reshape(cols, P).T], axis=1))


def gnn_program(nc, step_c, x, src, dst, edge_attr, W_fc, b_fc, W_res, b_res,
                Wm1, bm1, We1, be1, Ws1, bs1, Wm2, bm2, We2, be2, Ws2, bs2, out):
    N, D = x.shape
    E = src.shape[0]
    assert (N, E) == (N_NODES, N_EDGES)
    T = E // P
    FULL, REST = N // P, N % P
    NPAD = BLOCKS * P
    B0 = REGIONS[0][0]
    DB = BLOCKS - B0
    ITERS = DB // 2
    D0 = B0 * P
    REG, CSTEPS = regions()
    CG = -(-CSTEPS // P)
    HIS = BLOCKS
    WIN = HIS * WD
    HALF = HIS // 2
    G = 8
    SG = -(-(T + BLOCKS - 1) // P)
    SPAD = SG * P
    BESIDE = DB * G
    TP, TC = 125, T // 125
    EG = 5
    GROUPS = T // EG
    EB = 8
    LAG = 3
    ESTEPS = -(-(GROUPS + BLOCKS - 1) // EB) * EB
    ES = -(-(ESTEPS + 1) // P)
    NB = 7
    NITER = BLOCKS // NB
    F1 = D + 1
    FAR = 1.0e6
    NEVER = 1 << 14
    CW = CG * P
    PIECES = 8
    HB, RING = 4, 8
    YW = BLOCKS * 3 * D // 2
    UNION = 2 * CW + RING * (P + WIN) // 2
    PATH = SPAD + 2 * ES * P + P
    MORE = (SPAD - BESIDE) // (2 * G)
    BG, BC = -(-SG // 4), -(-CG // 4)
    BE = -(-TC // 4)
    assert TP * TC == T and GROUPS * EG == T and BLOCKS % NB == 0
    assert 3 * CG >= 64 and 4 * CG >= BLOCKS
    assert UNION >= YW >= BLOCKS * F1 and B0 >= 2 and WPB % HB == 0
    assert all(n % 2 == 0 for _, n, _, _ in REG) and HIS % 2 == 0 and SPAD >= T + BLOCKS - 1 + 2 * G

    ctx = ExitStack()
    with ctx:
        def sb(name, shape, dt=F32):
            return ctx.enter_context(nc.sbuf_tensor(name, shape, dt))

        def sem(name):
            return ctx.enter_context(nc.semaphore(name))

        def sems(name, n):
            return [sem(f"{name}{i}") for i in range(n)]

        x_pad = nc.dram_tensor("x_pad", [NPAD, D], F32).ap()
        x1_tab = nc.dram_tensor("x1_tab", [NPAD, D], F32).ap()
        y_tab = nc.dram_tensor("y_tab", [NPAD, 3 * D], BF16).ap()
        a_dram = [nc.dram_tensor(f"a_dram{j}", [ITERS, 2, P, HALF * P], F16).ap() for j in range(2)]
        left_dram = nc.dram_tensor("left_dram", [T, P], F32).ap()
        last_dram = nc.dram_tensor("last_dram", [T], I32).ap()
        need_dram = nc.dram_tensor("need_dram", [T], F32).ap()
        path_dram = nc.dram_tensor("path_dram", [PATH], I16).ap()
        base_dram = nc.dram_tensor("base_dram", [ES * P], F32).ap()

        acc = sb("acc", [P, BLOCKS, D])
        early = sb("early", [P, YW])
        msg = sb("msg", [P, 2 * G, 3 * D], BF16)
        abuf = sb("abuf", [P, 2, HIS * P], F16)
        union = sb("union", [P, UNION])
        code_g = sb("code_g", [P, SPAD], F16)
        src_g = sb("src_g", [P, SPAD], I16)
        path = sb("path", [1, G + PATH], I16)
        base_e = sb("base_e", [P, ES * P])
        ident = sb("ident", [P, P])
        lane16 = sb("lane16", [P, WIN], F16)
        lanef = sb("lanef", [P, P])
        epst = sb("epst", [P, 1])
        zpad = sb("zpad", [P - REST, D])
        idx = sb("idx", [P, 2 * G], I32)
        hot_g = sb("hot_g", [P, 2 * G, P], F16)
        part_d = sb("part_d", [P, 2, D])
        step_no = sb("step_no", [P, SG])
        sc = sb("sc", [P, 2, CG])
        small = sb("small", [P, 19, CG])
        gidx = sb("gidx", [P, 3, CG], I32)
        rdeg = sb("rdeg", [P, BLOCKS])
        w_in = sb("w_in", [F1, 2, D])
        w_ys = sb("w_ys", [F1, 3, 2, D])
        w_e = sb("w_e", [D, 2, D])
        bme = sb("bme", [P, 2, 2, D])
        mean = sb("mean", [P, NB])
        sdev = sb("sdev", [P, NB])
        ps = ctx.enter_context(nc.psum_tensor("ps", [P, 8, 512], F32))

        af = abuf[:, :, :].rearrange("p a c -> p (a c)").bitcast(F32)
        accf = acc[:, :, :].rearrange("p b d -> p (b d)")
        easf = early[:, :]
        eas = early[:, 0:BLOCKS * F1].rearrange("p (b d) -> p b d", d=F1)
        smallf = small[:, :, :].rearrange("p a b -> p (a b)")
        code_h, code_l = union[:, 0:CW], union[:, CW:2 * CW]
        hot_c = union[:, 2 * CW:UNION].bitcast(F16).rearrange("p (s c) -> p s c", s=RING)
        y_of = [early[:, :], union[:, 0:YW], union[:, 0:YW]]
        yparts = [t.bitcast(BF16).rearrange("p (b c d) -> p b c d", c=3, d=D) for t in y_of]
        ycols = [t.bitcast(BF16).rearrange("p (b c) -> p b c", c=3 * D) for t in y_of]
        TW = TC * P
        dtf = [*(af[0:TP, k * TW:(k + 1) * TW] for k in range(3)), union[0:TP, 0:TW]]
        dtm = [t.bitcast(I32) for t in dtf]
        wtm = accf[0:TP, 0:TW].bitcast(I32)
        unc = easf[0:TP, 0:TW]
        needt = easf[0:TP, TW:TW + TC]
        lastt = easf[0:TP, TW + TC:TW + 2 * TC].bitcast(I32)
        last_b = af[:, 0:T].bitcast(I32)
        leave_b, taken_b, need_b = (af[:, k * T:(k + 1) * T] for k in (1, 2, 3))
        junk, last16 = accf[:, 0:T], accf[:, T:2 * T].bitcast(I16)[:, 0:T]
        leave16, taken16 = (af[:, 0:T].bitcast(I16)[:, k * T:(k + 1) * T] for k in range(2))
        hits = easf[:, 0:T].bitcast(F16)[:, 0:T]
        ones_g, leave_e = easf[:, T:T + GROUPS], easf[:, 2 * T:2 * T + GROUPS].bitcast(I16)[:, 0:GROUPS]
        rows_gd, rows_gs = af[:, 0:SPAD], af[:, SPAD:2 * SPAD].bitcast(I32)
        rows_ct = af[:, 2 * SPAD:2 * SPAD + CW].bitcast(I32)
        before_ct = af[:, 2 * SPAD:2 * SPAD + CW]
        rows_cd, rows_cs = code_h.bitcast(I32), code_l.bitcast(I32)
        at = [0]

        def carve(n):
            at[0] += n
            assert at[0] <= HIS * P
            return af[:, at[0] - n:at[0]]

        dst_e = carve(EG * GROUPS).rearrange("p (g j) -> p g j", j=EG)
        dst_rows = carve(TW)[0:TP, :]
        feats = union[:, 0:EB * EG * D].rearrange("p (s j d) -> p s j d", s=EB, d=D)
        rests = union[:, EB * EG * D:2 * EB * EG * D].rearrange("p (s j d) -> p s j d", s=EB, d=D)
        EPW = -(-EG * 3 * F1 // 2)
        parts = [union[:, 2 * EB * EG * D + h * EPW:2 * EB * EG * D + (h + 1) * EPW].bitcast(BF16)[:, 0:EG * 3 * F1]
                 for h in range(EB)]
        assert 2 * EB * EG * D + EB * EPW <= UNION
        parts4 = [v.rearrange("p (j c d) -> p j c d", c=3, d=F1) for v in parts]
        hot_e = carve(EB * EG * P // 2).bitcast(F16).rearrange("p (s j c) -> p s j c", s=EB, c=P)
        NEXT = 4 * NB * D + 2 * NB * P
        nrows = [af[:, c:c + NB * D].rearrange("p (b d) -> p b d", d=D) for c in (0, NEXT)]
        feat = af[:, NB * D:2 * NB * D].rearrange("p (b d) -> p b d", d=D)
        t2 = af[:, 2 * NB * D:3 * NB * D].rearrange("p (b d) -> p b d", d=D)
        xT = af[0:F1, 3 * NB * D:3 * NB * D + NB * P]
        eT = af[0:D, 3 * NB * D + NB * P:3 * NB * D + 2 * NB * P]
        ecopy = af[:, 3 * NB * D + 2 * NB * P:4 * NB * D + 2 * NB * P].rearrange("p (b d) -> p b d", d=D)
        regs = smallf[:, 11 * CG:11 * CG + 64]
        trT = sb("trT", [64, P], I16)[:, :]
        trF = sb("trF", [64, P])[:, :]
        mu, root = smallf[:, 0:BLOCKS], smallf[:, 4 * CG:4 * CG + BLOCKS]

        s_const = sem("s_const")
        s_v = sem("s_v")
        s_zero = sem("s_zero")
        s_w = sem("s_w")
        s_ld = sems("s_ld", 4)
        s_st = sems("s_st", 3)
        s_bc = sems("s_bc", 2)
        s_lde = sem("s_lde")
        s_xpad = sem("s_xpad")
        s_g = sems("s_g", 5)
        s_pt = sem("s_pt")
        s_pc = sem("s_pc")
        s_path = sem("s_path")
        s_path_in = sem("s_path_in")
        e_in = sems("e_in", EB)
        e_one = sems("e_one", EB)
        e_rem = sems("e_rem", EB)
        e_two = sems("e_two", EB)
        e_three = sems("e_three", EB)
        e_hot = sems("e_hot", EB)
        e_mm = sems("e_mm", EB)
        e_add = sem("e_add")
        made = sem("made")
        stepped = sem("stepped")
        evacd = sem("evacd")
        b_used = sems("b_used", 2)
        b_red = sems("b_red", 2)
        stored = sems("stored", 2)
        a_in = [sems(f"a_in{j}_", 2) for j in range(2)]
        a_used = [sems(f"a_used{j}_", 2) for j in range(2)]
        d_red = sems("d_red", 2)
        staged = [sems(f"staged{r}_", 2) for r in range(3)]
        claimed = sem("claimed")
        gathered = [sems(f"gathered{r}_", 2) for r in range(3)]
        marked = [sems(f"marked{r}_", 2) for r in range(3)]
        gsum = [sems(f"gsum{r}_", 2) for r in range(3)]
        gred = [sems(f"gred{r}_", 2) for r in range(3)]
        s_add = sems("s_add", 3)
        round_done = sem("round_done")
        n_in = sem("n_in")
        n_t = sem("n_t")
        n_c = sem("n_c")
        n_v = sem("n_v")
        sp_turn = sem("sp_turn")
        n_turn = sem("n_turn")
        e_turn = sem("e_turn")
        n_eas = sems("n_eas", 2)
        s_ones = sem("s_ones")
        x1_st = sem("x1_st")
        y_st = sem("y_st")
        s_fin = sem("s_fin")
        s_root = sem("s_root")
        s_out = sem("s_out")

        block = ctx.enter_context(nc.Block())
        mark = {}

        START = 20
        NV, FEAT, NT, NC = (5, 18, 9), (0, 11, 1), (2, 5, 3), (1, 4, 2)
        vb = [START + NITER * sum(NV[:r]) for r in range(4)]
        tb = [NITER * sum(NT[:r]) for r in range(4)]
        cb = [NITER * sum(NC[:r]) for r in range(4)]

        def load(engine, frm, n, top, skip=G):
            _, v = nc.values_load_multi_w_load_instructions(
                path[0:1, bass.ds(frm + skip, n)], engines=(engine,), min_val=0, max_val=top,
                skip_runtime_bounds_check_because="clamped to this range when the path was made")
            return v

        def flat(v):
            return v.rearrange("p b d -> p (b d)")

        @block.vector
        def _(dve):
            V = nc.vector
            count = [0]

            def step(ins, name=None):
                count[0] += 1
                ins.then_inc(s_v, 1)
                dve.wait_ge(s_v, count[0])
                if name:
                    mark[name] = count[0]

            V.memset(path[0:1, 0:G], 0).then_inc(s_zero, 1)
            V.memset(w_ys[D:F1, :, :, :], 0.0).then_inc(s_zero, 1)
            dve.sem_inc(e_add, EB)
            for free in [*d_red, *b_red, *(y for z in gred for y in z), *s_add]:
                dve.sem_inc(free, 1)
            dve.sem_inc(n_v, START)
            dve.wait_ge(s_const, CONSTS)
            for k in (1, 2, 3):
                step(V.memset(dtm[k][0:1, 0:k * P], -1000))
            dve.wait_ge(stored[0], 16)
            step(V.tensor_single_scalar(wtm, dtm[0], 2, op=ALU.arith_shift_right))
            for k in (1, 2, 3):
                dve.wait_ge(s_ld[k], 16 if k == 1 else 32)
                if k == 1:
                    dve.wait_ge(stored[1], 16)
                step(V.tensor_single_scalar(dtm[k], dtm[k], 2, op=ALU.arith_shift_right))
                step(V.tensor_tensor(dtf[k], dtm[k], wtm, ALU.is_equal))
            step(V.tensor_scalar(unc, dtm[0], float(D0), None, ALU.is_lt))
            for b, k in REGIONS:
                step(V.scalar_tensor_tensor(dtf[k], dtm[0], float(b * P), dtf[k], ALU.is_ge, ALU.mult))
                step(V.tensor_tensor(unc, unc, dtf[k], ALU.max))
            step(V.tensor_reduce(needt, unc.rearrange("p (t e) -> p t e", e=P), AX.X, ALU.max))
            step(V.tensor_copy(lastt, dtm[0].rearrange("p (t e) -> p t e", e=P)[:, :, P - 1]))
            step(V.scalar_tensor_tensor(dtf[1], unc, -FAR, dtm[0], ALU.mult, ALU.add))
            step(V.tensor_scalar(dtf[1], dtf[1], FAR, None, ALU.add), "left")
            dve.wait_ge(s_bc[0], 16)
            dve.wait_ge(s_bc[1], 16)
            step(V.tensor_copy(last16, last_b))
            step(V.memset(junk, 1.0))
            step(V.tensor_tensor_scan(taken_b, junk, need_b, 0.0, ALU.mult, ALU.add))
            step(V.tensor_single_scalar(last_b, last_b, P.bit_length() - 1, op=ALU.arith_shift_right))
            step(V.scalar_tensor_tensor(leave_b, taken_b, -1.0, last_b, ALU.add, ALU.add))
            n_more = smallf[:, 15 * CG:15 * CG + 1]
            step(V.scalar_tensor_tensor(junk, leave_b, 1.0, need_b, ALU.add, ALU.mult))
            step(V.tensor_reduce(n_more, junk, AX.X, ALU.max))
            step(V.tensor_scalar(n_more, n_more, float(2 * G - 1 - BESIDE), 0.0, ALU.add, ALU.max))
            step(V.tensor_copy(gidx[:, 0, 0:1], n_more))
            step(V.tensor_single_scalar(gidx[:, 0, 0:1], gidx[:, 0, 0:1], (2 * G).bit_length() - 1,
                                        op=ALU.arith_shift_right))
            step(V.tensor_copy(n_more, gidx[:, 0, 0:1]))
            step(V.tensor_scalar(need_b, need_b, -float(NEVER), float(NEVER), ALU.mult, ALU.add))
            step(V.tensor_tensor(taken16, leave_b, need_b, ALU.add))
            step(V.tensor_copy(leave16, leave_b))
            by_step = lambda t: t.rearrange("p (g e) -> p g e", e=P)
            over = lambda t, n: t.unsqueeze(2).to_broadcast([P, n, P])
            for g in range(CG):
                step(V.tensor_scalar(hits, last16, sc[:, 0, g:g + 1], 0.0, ALU.is_lt, ALU.add,
                                     accum_out=small[:, 5, g:g + 1]))
            step(V.tensor_scalar(small[:, 6, :], small[:, 5, :], float(T - 1), None, ALU.min))
            step(V.tensor_copy(gidx[:, 1, :], small[:, 6, :]), "c_tile")
            left_n, taken_n, blk_n, past_n, base_n = (small[:, k, 0:SG] for k in range(5))
            for g in range(SG):
                step(V.tensor_scalar(hits, leave16, step_no[:, g:g + 1], 0.0, ALU.is_lt, ALU.add,
                                     accum_out=small[:, 0, g:g + 1]))
            dve.wait_ge(s_g[2], 16 * CG)
            step(V.tensor_tensor(by_step(before_ct), by_step(rows_ct), over(sc[:, 0, :], CG), ALU.is_lt))
            step(V.tensor_reduce(small[:, 16, :], by_step(before_ct), AX.X, ALU.add))
            step(V.scalar_tensor_tensor(small[:, 17, :], small[:, 6, :], float(P), small[:, 16, :],
                                        ALU.mult, ALU.add))
            step(V.tensor_tensor(small[:, 17, :], small[:, 17, :], sc[:, 1, :], ALU.add))
            step(V.tensor_scalar(small[:, 18, :], small[:, 17, :], float(E - P), None, ALU.min))
            step(V.tensor_copy(gidx[:, 2, :], small[:, 18, :]), "c_idx")
            for g in range(SG):
                step(V.tensor_scalar(hits, taken16, step_no[:, g:g + 1], 0.0, ALU.is_lt, ALU.add,
                                     accum_out=small[:, 1, g:g + 1]))
            step(V.tensor_scalar(blk_n, left_n, float(T - 1), None, ALU.min))
            step(V.tensor_copy(gidx[:, 0, 0:SG], blk_n))
            step(V.tensor_tensor(blk_n, step_no[:, :], taken_n, ALU.subtract))
            step(V.tensor_scalar(blk_n, blk_n, float(BLOCKS - 1), None, ALU.min))
            step(V.tensor_scalar(past_n, left_n, float(T), -FAR, ALU.is_ge, ALU.mult))
            step(V.scalar_tensor_tensor(base_n, blk_n, float(P), past_n, ALU.mult, ALU.add), "g_idx")
            last_of = last16.rearrange("p (g j) -> p g j", j=EG)[:, :, EG - 1]
            step(V.tensor_copy(junk[:, 0:GROUPS].bitcast(I32), last_of))
            step(V.tensor_single_scalar(junk[:, 0:GROUPS].bitcast(I32), junk[:, 0:GROUPS].bitcast(I32),
                                        P.bit_length() - 1, op=ALU.arith_shift_right))
            step(V.memset(ones_g, 1.0))
            step(V.tensor_tensor_scan(leave_e, ones_g, ones_g, -1.0, ALU.mult, ALU.add))
            step(V.tensor_tensor(leave_e, leave_e, junk[:, 0:GROUPS].bitcast(I32), ALU.add))
            e_left, e_grp, e_blk, e_base = (small[:, k, 0:ES] for k in range(7, 11))
            for g in range(ES):
                step(V.tensor_scalar(hits[:, 0:GROUPS], leave_e, step_no[:, g:g + 1], 0.0, ALU.is_lt, ALU.add,
                                     accum_out=small[:, 7, g:g + 1]))
            step(V.tensor_scalar(e_grp, e_left, float(GROUPS - 1), None, ALU.min))
            step(V.tensor_tensor(e_blk, step_no[:, 0:ES], e_left, ALU.subtract))
            step(V.tensor_scalar(e_blk, e_blk, float(BLOCKS - 1), None, ALU.min))
            step(V.tensor_scalar(e_base, e_left, float(GROUPS), -FAR, ALU.is_ge, ALU.mult))
            step(V.scalar_tensor_tensor(e_base, e_blk, float(P), e_base, ALU.mult, ALU.add))
            step(V.memset(regs, 0.0))
            for frm, to in ((blk_n, 0), (e_grp, 32), (e_blk, 40), (e_base, 48), (n_more, 56)):
                step(V.tensor_copy(regs[:, to:to + frm.shape[-1]], frm), "path")
            dve.wait_ge(s_g[0], 16 * SG)
            step(V.tensor_tensor(by_step(accf[:, 0:SPAD]), by_step(rows_gd), over(base_n, SG), ALU.subtract))
            step(V.tensor_scalar(accf[:, 0:SPAD], accf[:, 0:SPAD], -1.0, float(P), ALU.max, ALU.min), "rel_g")
            dve.wait_ge(s_g[1], 16 * SG)
            step(V.tensor_copy(easf[:, 0:SPAD], rows_gs), "src_g")
            dve.wait_ge(s_pc, 1 + 2 * BG)
            rel, tmp = accf[:, 0:CW], easf[:, 0:CW]
            step(V.tensor_tensor(small[:, 3, :], small[:, 17, :], small[:, 18, :], ALU.subtract))
            step(V.tensor_tensor(by_step(tmp), lanef[:, :].unsqueeze(1).to_broadcast([P, CG, P]),
                                 over(small[:, 3, :], CG), ALU.is_lt))
            dve.wait_ge(s_g[3], 16 * CG)
            step(V.tensor_tensor(by_step(rel), by_step(rows_cd), over(sc[:, 0, :], CG), ALU.subtract))
            step(V.scalar_tensor_tensor(tmp, rel, float(WD), tmp, ALU.is_ge, ALU.add))
            step(V.scalar_tensor_tensor(tmp, rel, 0.0, tmp, ALU.is_lt, ALU.add))
            step(V.scalar_tensor_tensor(rel, tmp, FAR, rel, ALU.mult, ALU.add))
            dve.wait_ge(s_g[4], 16 * CG)
            step(V.tensor_single_scalar(rows_cd, rows_cs, P.bit_length() - 1, op=ALU.arith_shift_right))
            step(V.scalar_tensor_tensor(rel, rows_cd, float(WD), rel, ALU.mult, ALU.add), "code_h")
            step(V.tensor_single_scalar(rows_cs, rows_cs, P - 1, op=ALU.bitwise_and))
            step(V.tensor_copy(tmp, rows_cs), "code_l")
            dve.wait_ge(s_pc, 1 + 2 * BG + 2 * BC)
            step(V.memset(acc[:, :, :], 0.0))
            dve.wait_ge(s_w, 16 * LOADS)
            for c in range(2):
                step(V.tensor_tensor(bme[:, c, 0, :], bme[:, c, 0, :], bme[:, c, 1, :], ALU.add))
            dve.wait_ge(s_path_in, 32)
            dve.wait_ge(s_zero, 2)
            step(V.memset(abuf[:, 1, :], 0.0), "prepared")
            for r in range(3):
                V.memset(xT[D:F1, :], 1.0).then_inc(s_ones, 1)
                with dve.Fori(0, NITER // 2) as pair:
                    for half in range(2):
                        i = pair * 2 + half
                        n = [0]

                        def vstep(ins):
                            n[0] += 1
                            ins.then_inc(n_v, 1)
                            dve.wait_ge(n_v, i * NV[r] + (n[0] + vb[r]))

                        blk = bass.ds(i * NB, NB)
                        bc = lambda t: t.unsqueeze(2).to_broadcast([P, NB, D])
                        prod = [ps[:, 2:4, :].rearrange("p k c -> p (k c)")[:, 0:NB * 2 * D]
                                .rearrange("p (b c d) -> p b c d", c=2, d=D)[:, :, c, :] for c in range(2)]
                        if r:
                            dve.wait_ge(n_in, i * 16 + (16 + 16 * NITER * r))
                        if r == 1:
                            vstep(V.tensor_tensor(t2, acc[:, blk, :], bc(rdeg[:, blk]), ALU.mult))
                            dve.wait_ge(n_t, i * NT[r] + (3 + tb[r]))
                            vstep(V.tensor_tensor(t2, t2, prod[0], ALU.add))
                            vstep(V.scalar_tensor_tensor(t2, t2, 0.0, prod[1], ALU.max, ALU.add))
                            vstep(V.tensor_tensor(t2, t2, nrows[half], ALU.add))
                            vstep(V.tensor_reduce(mean[:, :], t2, AX.X, ALU.add))
                            vstep(V.tensor_scalar(mean[:, :], mean[:, :], 1.0 / D, None, ALU.mult))
                            vstep(V.tensor_tensor(t2, t2, bc(mean[:, :]), ALU.subtract))
                            vstep(V.tensor_tensor(feat, t2, t2, ALU.mult))
                            vstep(V.tensor_reduce(mean[:, :], feat, AX.X, ALU.add))
                            dve.wait_ge(n_c, i * NC[r] + (3 + cb[r]))
                            vstep(V.reciprocal(sdev[:, :], sdev[:, :]))
                            vstep(V.tensor_tensor(feat, t2, bc(sdev[:, :]), ALU.mult))
                        elif r == 2:
                            vstep(V.tensor_scalar(feat, acc[:, blk, :], 0.0, None, ALU.max))
                        assert n[0] == FEAT[r]
                        dve.wait_ge(n_t, i * NT[r] + (NT[r] + tb[r]))
                        y = [yparts[r][:, blk, c, :] for c in range(3)]
                        vstep(V.tensor_copy(y[0], prod[0]))
                        vstep(V.tensor_tensor(t2, prod[0], y[0], ALU.subtract))
                        vstep(V.tensor_copy(y[1], t2))
                        vstep(V.tensor_tensor(t2, t2, y[1], ALU.subtract))
                        vstep(V.tensor_copy(y[2], t2))
                        if r:
                            vstep(V.tensor_tensor(t2, bme[:, r - 1, 0, :].unsqueeze(1).to_broadcast([P, NB, D]),
                                                  eas[:, blk, D:F1].to_broadcast([P, NB, D]), ALU.mult))
                            vstep(V.tensor_tensor(acc[:, blk, :], t2, prod[1], ALU.add))
                            if r == 2:
                                vstep(V.tensor_tensor(acc[:, blk, :], acc[:, blk, :], nrows[half], ALU.add))
                        if r == 1:
                            dve.wait_ge(x1_st, i * 16 + 16)
                        assert n[0] == NV[r]

                def g_mark(it, j):
                    dve.wait_ge(gsum[r][j], it + 1)
                    V.tensor_tensor(hot_g[:, j * G:(j + 1) * G, :],
                                    code_g[:, bass.ds((it * 2 + j) * G, G)].unsqueeze(2).to_broadcast([P, G, P]),
                                    lane16[:, 0:P].unsqueeze(1).to_broadcast([P, G, P]), ALU.is_equal)\
                        .then_inc(marked[r][j], 1)

                def g_add(it, j, before):
                    bs = load(ENG.DVE, (it * 2 + j) * G, G, BLOCKS - 1)
                    dve.wait_ge(gsum[r][j], it + 2)
                    for k in range(G):
                        to = flat(acc[:, bass.ds(bs[k], 1), :])
                        V.tensor_tensor(to, to, ps[:, 6 + j, k * D:(k + 1) * D], ALU.add).then_inc(s_add[r], 1)
                        dve.wait_ge(s_add[r], before + (k + 1))
                    dve.sem_inc(gred[r][j], 1)

                if r == 0:
                    step(V.memset(ps[:, 4, :], 0.0))
                    step(V.memset(ps[:, 7, :], 0.0), "zeros")
                    for b0, blocks, K, s0 in REG:
                        with dve.Fori(0, blocks // 2) as i:
                            for j in range(2):
                                it = i + b0 // 2
                                g_mark(it, j)
                                for q in range(WPB * K):
                                    n, s = q % RING, bass.ds(i * (2 * WPB * K) + (j * WPB * K + q + s0), 1)
                                    if q % HB == 0:
                                        dve.wait_ge(stepped, i * (2 * WPB * K) + (j * WPB * K + q + s0 + 1))
                                    V.tensor_scalar(hot_c[:, n, 0:WIN], lane16[:, :], code_h[:, s], None,
                                                    ALU.is_equal)
                                    last = V.tensor_scalar(hot_c[:, n, WIN:WIN + P], lane16[:, 0:P], code_l[:, s],
                                                           None, ALU.is_equal)
                                    if q % HB == HB - 1:
                                        last.then_inc(made, 1)
                                    part, odd = divmod(q - 8 * K, 2 * K)
                                    if part < 0 or odd or part > G + 2:
                                        continue
                                    before = it * (2 * (G + 1)) + (1 + j * (G + 1))
                                    if part == 0:
                                        bs = load(ENG.DVE, (it * 2 + j) * G, G, BLOCKS - 1, skip=0)
                                        dve.wait_ge(b_used[j], it + (1 + j))
                                        V.tensor_reduce(part_d[:, j, :],
                                                        ps[:, 4 + j, 0:3 * D].rearrange("p (c d) -> p d c", c=3),
                                                        AX.X, ALU.add).then_inc(b_red[j], 1)
                                    elif part == 1:
                                        dve.wait_ge(b_red[j], it + 2)
                                        to = flat(acc[:, bass.ds(i * 2 + (b0 + B0 + j - 2), 1), :])
                                        V.tensor_tensor(to, to, part_d[:, j, :], ALU.add).then_inc(s_add[0], 1)
                                    else:
                                        k = part - 2
                                        dve.wait_ge(s_add[0], before + (k + 1))
                                        if k == 0:
                                            dve.wait_ge(gsum[0][1 - j], it + (1 + j))
                                        if k < G:
                                            to = flat(acc[:, bass.ds(bs[k], 1), :])
                                            V.tensor_tensor(to, to, ps[:, 7 - j, k * D:(k + 1) * D], ALU.add)\
                                                .then_inc(s_add[0], 1)
                                        else:
                                            dve.sem_inc(gred[0][1 - j], 1)
                    for j in range(2):
                        dve.wait_ge(b_used[j], ITERS + 1 + j)
                        V.tensor_reduce(part_d[:, j, :], ps[:, 4 + j, 0:3 * D].rearrange("p (c d) -> p d c", c=3),
                                        AX.X, ALU.add).then_inc(b_red[j], 1)
                        dve.wait_ge(b_red[j], ITERS + 2)
                        to = acc[:, BLOCKS - 2 + j, :]
                        V.tensor_tensor(to, to, part_d[:, j, :], ALU.add).then_inc(s_add[0], 1)
                        dve.wait_ge(s_add[0], DB * (G + 1) + 2 + j)
                    g_add(ITERS - 1, 1, DB * (G + 1) + 3)
                    for j in range(2):
                        dve.wait_ge(stored[j], 16 * (ITERS + 1))

                if r:
                    with dve.Fori(0, ITERS) as i:
                        for j in range(2):
                            g_mark(i, j)
                            dve.wait_ge(a_used[j][1], i + (2 + (r - 1) * ITERS))
                            V.tensor_reduce(part_d[:, j, :], ps[:, 4 + j, 0:3 * D].rearrange("p (c d) -> p d c", c=3),
                                            AX.X, ALU.add).then_inc(d_red[j], 1)
                            dve.wait_ge(d_red[j], i + (2 + (r - 1) * ITERS))
                            before = i * (2 * (G + 1)) + (1 + j * (G + 1))
                            to = flat(acc[:, bass.ds(i * 2 + (B0 + j), 1), :])
                            V.tensor_tensor(to, to, part_d[:, j, :], ALU.add).then_inc(s_add[r], 1)
                            dve.wait_ge(s_add[r], before + 1)
                            g_add(i, j, before + 1)
                more = load(ENG.DVE, PATH - P, 1, MORE)[0]
                with dve.If(more > 0):
                    with dve.Fori(0, more) as i:
                        for j in range(2):
                            g_mark(i + ITERS, j)
                            g_add(i + ITERS, j, i * (2 * G) + (1 + DB * (G + 1) + (0 if r else G + 2) + j * G))
                dve.sem_inc(round_done, 1)
                if r:
                    continue

                dve.wait_ge(s_lde, 16)
                step(V.tensor_copy(dst_rows, dst_rows.bitcast(I32)), "dst_e")
                dve.wait_ge(s_pc, 1 + 2 * BG + 2 * BC + BE)
                step(V.memset(eas[:, :, :], 0.0))
                for v in parts4:
                    step(V.memset(v[:, :, :, D:F1], 0.0))
                    step(V.memset(v[:, :, 0, D:F1], 1.0), "ones_e")

                step(V.memset(ps[:, EB - LAG:EB, 0:F1], 0.0), "zeros_e")
                with dve.Fori(0, ESTEPS // EB) as i:
                    grp = load(ENG.DVE, i * EB + (SPAD + ES * P), EB, GROUPS - 1)
                    bs = load(ENG.DVE, i * EB + SPAD, EB, BLOCKS - 1, skip=G - LAG)
                    for h in range(EB):
                        dve.wait_ge(e_mm[h], i + 1)
                        V.scalar_tensor_tensor(hot_e[:, h, :, :],
                                               flat(dst_e[:, bass.ds(grp[h], 1), :]).unsqueeze(2).to_broadcast([P, EG, P]),
                                               base_e[:, bass.ds(i * EB + h, 1)],
                                               lane16[:, 0:P].unsqueeze(1).to_broadcast([P, EG, P]),
                                               ALU.subtract, ALU.is_equal).then_inc(e_hot[h], 1)
                        if h % 2:
                            dve.wait_ge(e_two[h], i + 1)
                            V.tensor_tensor(parts4[h][:, :, 2, 0:D], rests[:, h, :, :], parts4[h][:, :, 1, 0:D],
                                            ALU.subtract).then_inc(e_three[h], 1)
                        b = (h - LAG) % EB
                        dve.wait_ge(e_mm[b], i + (2 if h >= LAG else 1))
                        dve.wait_ge(e_add, i * EB + (h + EB))
                        to = flat(eas[:, bass.ds(bs[h], 1), :])
                        V.tensor_tensor(to, to, ps[:, b, 0:F1], ALU.add).then_inc(e_add, 1)
                last = load(ENG.DVE, SPAD + ESTEPS - LAG, LAG, BLOCKS - 1)
                for k in range(LAG):
                    dve.wait_ge(e_mm[EB - LAG + k], ESTEPS // EB + 1)
                    dve.wait_ge(e_add, ESTEPS + k + EB)
                    to = flat(eas[:, bass.ds(last[k], 1), :])
                    V.tensor_tensor(to, to, ps[:, EB - LAG + k, 0:F1], ALU.add).then_inc(e_add, 1)
                dve.wait_ge(e_add, ESTEPS + LAG + EB)
                step(V.tensor_scalar(rdeg[:, :], eas[:, :, D], 1.0, None, ALU.max))
                step(V.reciprocal(rdeg[:, :], rdeg[:, :]))
                dve.sem_inc(round_done, 1)

            fin = [0]

            def last_step(ins):
                fin[0] += 1
                ins.then_inc(s_fin, 1)
                dve.wait_ge(s_fin, fin[0])

            squares = union[:, 0:BLOCKS * D].rearrange("p (b d) -> p b d", d=D)
            wide = lambda t: t.unsqueeze(2).to_broadcast([P, BLOCKS, D])
            last_step(V.tensor_reduce(mu, acc[:, :, :], AX.X, ALU.add))
            last_step(V.tensor_scalar(mu, mu, 1.0 / D, None, ALU.mult))
            last_step(V.tensor_tensor(acc[:, :, :], acc[:, :, :], wide(mu), ALU.subtract))
            last_step(V.tensor_tensor(squares, acc[:, :, :], acc[:, :, :], ALU.mult))
            last_step(V.tensor_reduce(mu, squares, AX.X, ALU.add))
            dve.wait_ge(s_root, 1)
            last_step(V.reciprocal(root, root))
            last_step(V.tensor_tensor(acc[:, :, :], acc[:, :, :], wide(root), ALU.mult))

        jobs = [(mark["path"], [(regs, 64, P, trT)])]
        for frm, name, to, cols in ((accf, "rel_g", code_g, SG), (easf, "src_g", src_g, SG),
                                    (accf, "code_h", code_h, CG), (easf, "code_l", code_l, CG)):
            for g0 in range(0, cols, 4):
                jobs.append((mark[name], [(frm[:, g * P:(g + 1) * P], P, P, to[:, g * P:(g + 1) * P])
                                          for g in range(g0, min(g0 + 4, cols))]))
        e_src = dst_rows.rearrange("p (a q j) -> p a j q", a=TC // EG, j=EG)
        e_dst = dst_e.rearrange("p (q a) j -> p a j q", a=TC // EG)
        pieces = [(e_src[:, a, j, :], P, TP, e_dst[:, a, j, :]) for a in range(TC // EG) for j in range(EG)]
        for g0 in range(0, len(pieces), 4):
            jobs.append((mark["dst_e"], pieces[g0:g0 + 4]))
        assert len(jobs) == 1 + 2 * BG + 2 * BC + BE

        @block.tensor
        def _(pe):
            for free in [*e_mm, *b_used, *(y for z in a_used for y in z), *(y for z in gsum for y in z)]:
                pe.sem_inc(free, 1)
            pe.sem_inc(stepped, HB + 1)
            pe.wait_ge(s_const, CONSTS)

            def prepare(first, end):
                for n in range(first, end):
                    ready, items = jobs[n]
                    pe.wait_ge(s_v, ready)
                    if n >= 4:
                        pe.wait_ge(s_pc, n - 3)
                    for c, (frm, m, k, _) in enumerate(items):
                        last = pe.transpose(ps[0:m, n % 4, c * P:c * P + k], frm, ident[0:k, 0:k])
                    last.then_inc(s_pt, 1)

            prepare(0, len(jobs) - BE)
            for r in range(3):
                if r == 0:
                    pe.wait_ge(s_pc, len(jobs) - BE)
                else:
                    pe.wait_ge(round_done, r + 1)
                pe.wait_ge(s_ones, r + 1)
                pe.wait_ge(s_w, 16 * LOADS)
                with pe.Fori(0, NITER // 2) as pair:
                    for half in range(2):
                        i = pair * 2 + half
                        def turn(rows, first_bank):
                            for b in range(NB):
                                k = first_bank + b // 4
                                last = pe.transpose(ps[0:D, k, b % 4 * P:(b % 4 + 1) * P], rows(b), ident[:, :])
                            return last

                        def both(b):
                            return ps[:, 2 + b // 4, b % 4 * 2 * D:(b % 4 + 1) * 2 * D]

                        if r:
                            pe.wait_ge(n_eas[r - 1], i + 1)
                            pe.sem_inc(n_turn, 1)
                            turn(lambda b: ecopy[:, b, :], 4).then_inc(n_t, 1)
                        if r < 2:
                            pe.wait_ge(n_in, i * 16 + (16 + 16 * NITER * r))
                            pe.sem_inc(n_turn, 1)
                            turn(lambda b: nrows[half][:, b, :], 0).then_inc(n_t, 1)
                            pe.wait_ge(n_c, i * NC[r] + (1 + (r > 0) + cb[r]))
                        if r < 2:
                            pe.wait_ge(n_v, i * NV[r] + vb[r])
                            pe.sem_inc(n_turn, 1)
                        if r == 1:
                            for b in range(NB):
                                last = nc.tensor.matmul(both(b), xT[:, b * P:(b + 1) * P],
                                                        w_in[:, :, :].rearrange("f c d -> f (c d)"), start=True, stop=True)
                            last.then_inc(n_t, 1)
                        if r:
                            pe.wait_ge(n_v, i * NV[r] + (FEAT[r] + vb[r]))
                            pe.sem_inc(n_turn, 1)
                            turn(lambda b: feat[:, b, :], 0).then_inc(n_t, 1)
                            pe.wait_ge(n_c, i * NC[r] + (NC[r] + cb[r]))
                            for b in range(NB):
                                nc.tensor.matmul(both(b), xT[:, b * P:(b + 1) * P],
                                                 w_ys[:, r, :, :].rearrange("f c d -> f (c d)"), start=True, stop=False)
                                last = nc.tensor.matmul(both(b)[:, D:2 * D], eT[:, b * P:(b + 1) * P],
                                                        w_e[:, r - 1, :], start=False, stop=True)
                        else:
                            for b in range(NB):
                                last = nc.tensor.matmul(both(b)[:, 0:D], xT[0:D, b * P:(b + 1) * P],
                                                        w_ys[0:D, 0, 0, :], start=True, stop=True)
                        last.then_inc(n_t, 1)
                pe.wait_ge(n_v, vb[r + 1])

                def g_multiply(it, j):
                    pe.wait_ge(marked[r][j], it + 1)
                    pe.wait_ge(gathered[r][j], (it + 1) * (16 * G))
                    pe.wait_ge(gred[r][j], it + (1 if r else 1 + j))
                    for k in range(G):
                        s = j * G + k
                        for c in range(3):
                            last = nc.tensor.matmul(ps[:, 6 + j, k * D:(k + 1) * D], hot_g[:, s, :],
                                                    msg[:, s, c * D:(c + 1) * D], start=c == 0, stop=c == 2)
                    last.then_inc(gsum[r][j], 1)

                def dense(buffer, bank, h0, h1):
                    for hi in range(h0, h1):
                        last = nc.tensor.matmul(ps[:, bank, 0:3 * D], abuf[:, buffer, hi * P:(hi + 1) * P],
                                                ycols[r][:, hi, :], start=hi == 0, stop=hi == HIS - 1)
                    return last

                if r == 0:
                    pe.wait_ge(s_v, mark["zeros"])
                    for b0, blocks, K, s0 in REG:
                        with pe.Fori(0, blocks // 2) as i:
                            for j in range(2):
                                it = i + b0 // 2
                                for q in range(WPB * K):
                                    w, c = q // K, q % K
                                    if q % HB == 0:
                                        pe.wait_ge(made, i * (2 * WPB * K // HB) + ((j * WPB * K + q + s0) // HB + 1))
                                    if c == 0 and w % 2 == 0:
                                        pe.wait_ge(evacd, i * (2 * WPB) + ((b0 + j) * WPB + w + 1))
                                    n = q % RING
                                    nc.tensor.matmul(ps[:, w % 4, 0:WIN], hot_c[:, n, WIN:WIN + P],
                                                     hot_c[:, n, 0:WIN], start=c == 0, stop=c == K - 1)\
                                        .then_inc(stepped, 1)
                                    piece, odd = divmod(q + 1, WPB * K // PIECES)
                                    if odd:
                                        continue
                                    if piece == 1:
                                        pe.wait_ge(b_red[1 - j], it + (1 + j))
                                        pe.wait_ge(evacd, i * (2 * WPB) + ((b0 + j) * WPB + 3))
                                    last = dense(1 - j, 5 - j, HIS * (piece - 1) // PIECES, HIS * piece // PIECES)
                                last.then_inc(b_used[1 - j], 1)
                                g_multiply(it, j)
                    pe.wait_ge(b_red[1], ITERS + 1)
                    pe.wait_ge(evacd, DB * WPB + 3)
                    dense(1, 5, 0, HIS).then_inc(b_used[1], 1)

                if r:
                    with pe.Fori(0, ITERS) as i:
                        for j in range(2):
                            pe.wait_ge(d_red[j], i + (1 + (r - 1) * ITERS))
                            for u in range(2):
                                pe.wait_ge(a_in[j][u], i * 16 + 16 * (1 + (r - 1) * ITERS))
                                dense(j, 4 + j, u * HALF, (u + 1) * HALF).then_inc(a_used[j][u], 1)
                            g_multiply(i, j)
                more = load(ENG.PE, PATH - P, 1, MORE)[0]
                with pe.If(more > 0):
                    with pe.Fori(0, more) as i:
                        for j in range(2):
                            g_multiply(i + ITERS, j)
                if r == 0:
                    prepare(len(jobs) - BE, len(jobs))
                    pe.wait_ge(s_pc, len(jobs))
                    pe.wait_ge(s_v, mark["zeros_e"])
                    with pe.Fori(0, ESTEPS // EB) as i:
                        for h in range(EB):
                            pe.wait_ge(e_three[h], i + 1)
                            pe.wait_ge(e_hot[h], i + 1)
                            pe.wait_ge(e_add, i * EB + (h + LAG + 1))
                            for j in range(EG):
                                for c in range(3):
                                    last = nc.tensor.matmul(ps[:, h, 0:F1], hot_e[:, h, j, :], parts4[h][:, j, c, :],
                                                            start=j == c == 0, stop=(j, c) == (EG - 1, 2))
                            last.then_inc(e_mm[h], 1)

        @block.gpsimd
        def _(pool):
            for free in e_rem:
                pool.sem_inc(free, 1)
            pool.memset(zpad[:, :], 0.0).then_inc(s_const, 1)
            pool.memset(ident[:, :], 0.0).then_inc(s_const, 1)
            pool.iota(step_no[:, :], [[P, SG]], base=0, channel_multiplier=1,
                      allow_small_or_imprecise_dtypes=True).then_inc(s_const, 1)
            pool.iota(lane16[:, :], [[1, WIN]], base=0, channel_multiplier=0,
                      allow_small_or_imprecise_dtypes=True).then_inc(s_const, 1)
            pool.iota(lanef[:, :], [[1, P]], base=0, channel_multiplier=0,
                      allow_small_or_imprecise_dtypes=True).then_inc(s_const, 1)
            pool.memset(epst[:, :], EPS).then_inc(s_const, 1)
            pool.wait_ge(s_const, 2)
            pool.affine_select(out=ident[:, :], in_=ident[:, :], compare_op=ALU.not_equal, fill=1.0,
                               base=0, pattern=[[-1, P]], channel_multiplier=1).then_inc(s_const, 1)
            tiles = lambda a: a.rearrange("(t e) -> t e", e=P)
            single = lambda a: a.rearrange("(e o) -> e o", o=1)

            def fetch(rows, table, which, cols, done):
                for g in range(cols):
                    pool.indirect_dma_start(rows[:, g * P:(g + 1) * P], None, table, bass.IndirectOffsetOnAxis(
                        ap=gidx[:, which, g:g + 1], axis=0)).then_inc(done, 16)

            pool.wait_ge(s_v, mark["c_tile"])
            fetch(rows_ct, tiles(dst), 1, CG, s_g[2])
            pool.wait_ge(s_v, mark["c_idx"])
            fetch(rows_cd, single(dst), 2, CG, s_g[3])
            fetch(rows_cs, single(src), 2, CG, s_g[4])
            pool.wait_ge(s_v, mark["g_idx"])
            pool.wait_ge(s_st[0], 16)
            fetch(rows_gd, left_dram, 0, SG, s_g[0])
            fetch(rows_gs, tiles(src), 0, SG, s_g[1])
            for r in range(3):
                pool.wait_ge(y_st, 16 * NITER * (r + 1))

                def g_fetch(it, j):
                    pool.wait_ge(staged[r][j], it + 1)
                    pool.sem_inc(claimed, 1)
                    for k in range(G):
                        s = j * G + k
                        pool.indirect_dma_start(msg[:, s, :], None, y_tab, bass.IndirectOffsetOnAxis(
                            ap=idx[:, s:s + 1], axis=0)).then_inc(gathered[r][j], 16)

                with pool.Fori(0, ITERS) as i:
                    for j in range(2):
                        g_fetch(i, j)
                more = load(ENG.Pool, PATH - P, 1, MORE)[0]
                with pool.If(more > 0):
                    with pool.Fori(0, more) as i:
                        for j in range(2):
                            g_fetch(i + ITERS, j)
                if r == 0:
                    with pool.Fori(0, ESTEPS // EB) as i:
                        for t in range(EB + 2):
                            if t < EB:
                                pool.wait_ge(e_one[t], i + 1)
                                nc.gpsimd.tensor_tensor(rests[:, t, :, :], feats[:, t, :, :], parts4[t][:, :, 0, 0:D],
                                                        ALU.subtract).then_inc(e_rem[t], 1)
                            h = t - 2
                            if h >= 0 and h % 2 == 0:
                                pool.wait_ge(e_two[h], i + 1)
                                nc.gpsimd.tensor_tensor(parts4[h][:, :, 2, 0:D], rests[:, h, :, :],
                                                        parts4[h][:, :, 1, 0:D], ALU.subtract).then_inc(e_three[h], 1)

        @block.scalar
        def _(act):
            A = nc.scalar
            act.sem_inc(evacd, 3)

            def prepare(first, end):
                for n in range(first, end):
                    act.wait_ge(s_pt, n + 1)
                    if n == 0:
                        A.activation(trT, ps[0:64, 0, 0:P], ACT.Copy)
                        last = A.activation(trF, ps[0:64, 0, 0:P], ACT.Copy)
                    else:
                        for c, (_, m, k, to) in enumerate(jobs[n][1]):
                            last = A.activation(to, ps[0:m, n % 4, c * P:c * P + k], ACT.Copy)
                    last.then_inc(s_pc, 1)

            prepare(0, len(jobs) - BE)
            for r in range(3):
                if r:
                    act.wait_ge(round_done, r + 1)
                else:
                    act.wait_ge(s_v, mark["prepared"])
                    act.wait_ge(s_xpad, 32)
                if r == 2:
                    act.wait_ge(x1_st, 16 * NITER)
                rows = (x_pad, x_pad, x1_tab)[r].rearrange("(b p) d -> p b d", p=P)
                with act.Fori(0, NITER // 2) as pair:
                    for half in range(2):
                        i = pair * 2 + half
                        act.wait_ge(n_v, i * NV[r] + (vb[r] - NV[r]))
                        act.sem_inc(e_turn, 1)
                        act.dma_start(nrows[half], rows[:, bass.ds(i * NB, NB), :]).then_inc(n_in, 16)

                        def turned(to, k):
                            return A.activation(to, ps[0:D, k:k + 2, :].rearrange("p k c -> p (k c)")[:, 0:NB * P], ACT.Copy)

                        if r:
                            A.activation(ecopy, eas[:, bass.ds(i * NB, NB), 0:D], ACT.Copy).then_inc(n_eas[r - 1], 1)
                            act.wait_ge(n_t, i * NT[r] + (1 + tb[r]))
                            turned(eT, 4).then_inc(n_c, 1)
                        if r < 2:
                            act.wait_ge(n_t, i * NT[r] + (1 + (r > 0) + tb[r]))
                            turned(xT[0:D, :], 0).then_inc(n_c, 1)
                        if r == 1:
                            act.wait_ge(n_v, i * NV[r] + (9 + vb[r]))
                            A.activation(sdev[:, :], mean[:, :], ACT.Sqrt, bias=epst[:, :], scale=1.0 / D).then_inc(n_c, 1)
                        if r:
                            act.wait_ge(n_t, i * NT[r] + (NT[r] - 1 + tb[r]))
                            turned(xT[0:D, :], 0).then_inc(n_c, 1)

                def g_stage(it, j):
                    act.wait_ge(gsum[r][j], it + 1)
                    A.activation(idx[:, j * G:(j + 1) * G], src_g[:, bass.ds((it * 2 + j) * G, G)], ACT.Copy)\
                        .then_inc(staged[r][j], 1)

                if r:
                    with act.Fori(0, ITERS) as i:
                        for j in range(2):
                            g_stage(i, j)
                else:
                    act.wait_ge(n_v, vb[1])
                    for b0, blocks, K, s0 in REG:
                        with act.Fori(0, blocks // 2) as i:
                            for j in range(2):
                                g_stage(i + b0 // 2, j)
                                act.wait_ge(stored[j], i * 16 + 16 * (b0 // 2 + 1))
                                act.wait_ge(b_used[j], i + (b0 // 2 + 1 + j))
                                act.sem_inc(e_turn, 1)
                                for w in range(0, WPB, 2):
                                    act.wait_ge(stepped, i * (2 * WPB * K) + ((j * WPB + w + 2) * K + s0 + HB + 1))
                                    A.activation(abuf[:, j, :].rearrange("p (h w d) -> p w h d", w=WPB, d=WD)
                                                 [:, w:w + 2, :, :],
                                                 ps[:, w % 4:w % 4 + 2, 0:WIN].rearrange("p w (h d) -> p w h d", d=WD),
                                                 ACT.Copy).then_inc(evacd, 2)
                more = load(ENG.Activation, PATH - P, 1, MORE)[0]
                with act.If(more > 0):
                    with act.Fori(0, more) as i:
                        for j in range(2):
                            g_stage(i + ITERS, j)
                if r == 0:
                    prepare(len(jobs) - BE, len(jobs))
                    act.wait_ge(s_v, mark["ones_e"])
                    with act.Fori(0, ESTEPS // EB) as i:
                        for t in range(EB + 1):
                            if t < EB:
                                act.wait_ge(e_mm[t], i + 1)
                                act.wait_ge(e_in[t], i * 16 + 16)
                                act.sem_inc(e_turn, 1)
                                A.activation(parts4[t][:, :, 0, 0:D], feats[:, t, :, :], ACT.Copy)\
                                    .then_inc(e_one[t], 1)
                            if t:
                                act.wait_ge(e_rem[t - 1], i + 2)
                                A.activation(parts4[t - 1][:, :, 1, 0:D], rests[:, t - 1, :, :], ACT.Copy)\
                                    .then_inc(e_two[t - 1], 1)
            act.wait_ge(s_fin, 5)
            A.activation(root, mu, ACT.Sqrt, bias=epst[:, :], scale=1.0 / D).then_inc(s_root, 1)

        @block.sync
        def _(sp):
            sp.dma_start(dtm[0], dst.rearrange("(p c) -> p c", p=TP)).then_inc(stored[0], 16)
            for k in (1, 2, 3):
                a, b = TW - k * P, TW - k * P + (TP - 1) * TW
                sp.dma_start(dtm[k][1:TP, :], dst[a:b].rearrange("(p c) -> p c", p=TP - 1))\
                  .then_inc(stored[1] if k == 1 else s_ld[k], 16)
                sp.dma_start(dtm[k][0:1, k * P:TW], dst[0:a].rearrange("(p c) -> p c", p=1)).then_inc(s_ld[k], 16)
            row = lambda a: a.rearrange("(a n) -> a n", a=1)
            loads = [(sc[:, :, :], step_c), (w_in[0:D, 0, :], W_fc[0:D, :]), (w_in[0:D, 1, :], W_res),
                     (w_in[D:F1, 0, :], row(b_fc)), (w_in[D:F1, 1, :], row(b_res)), (w_ys[0:D, 0, 0, :], W_fc[D:2 * D, :])]
            for c, (wm, we, s_, bm, be, bs) in enumerate(((Wm1, We1, Ws1, bm1, be1, bs1),
                                                          (Wm2, We2, Ws2, bm2, be2, bs2))):
                loads += [(w_ys[0:D, 1 + c, 0, :], wm), (w_e[:, c, :], we), (w_ys[0:D, 1 + c, 1, :], s_),
                          (w_ys[D:F1, 1 + c, 1, :], row(bs)), (bme[:, c, 0, :], row(bm).to_broadcast([P, D])),
                          (bme[:, c, 1, :], row(be).to_broadcast([P, D]))]
            assert len(loads) == LOADS
            sp.wait_ge(s_zero, 2)
            for to, frm in loads:
                sp.dma_start(to, frm).then_inc(s_w, 16)
            sp.dma_start(x_pad[0:N, :], x).then_inc(s_xpad, 16)
            sp.wait_ge(s_const, 1)
            sp.dma_start(x_pad[N:NPAD, :], zpad[:, :]).then_inc(s_xpad, 16)
            sp.wait_ge(s_v, mark["left"])
            sp.dma_start(last_dram.rearrange("(p t) -> p t", p=TP), lastt).then_inc(s_st[1], 16)
            sp.dma_start(need_dram.rearrange("(p t) -> p t", p=TP), needt).then_inc(s_st[2], 16)
            sp.dma_start(left_dram.rearrange("(p t) e -> p (t e)", p=TP), dtf[1]).then_inc(s_st[0], 16)
            for k in range(3):
                sp.wait_ge(s_st[k], 16)
            sp.dma_start(last_b, row(last_dram).to_broadcast([P, T])).then_inc(s_bc[0], 16)
            sp.dma_start(need_b, row(need_dram).to_broadcast([P, T])).then_inc(s_bc[1], 16)
            sp.wait_ge(s_pc, 1)
            for frm, to, cols in ((0, 0, SG), (32, SPAD + ES * P, ES), (40, SPAD, ES), (56, PATH - P, 1)):
                sp.dma_start(path_dram[to:to + cols * P].rearrange("(g p) -> g p", p=P), trT[frm:frm + cols, :])\
                  .then_inc(s_path, 16)
            sp.dma_start(base_dram.rearrange("(g p) -> g p", p=P), trF[48:48 + ES, :]).then_inc(s_path, 16)
            sp.wait_ge(s_path, 80)
            sp.dma_start(path[:, G:G + PATH], row(path_dram)).then_inc(s_path_in, 16)
            sp.dma_start(base_e[:, :], row(base_dram).to_broadcast([P, ES * P])).then_inc(s_path_in, 16)
            for r in range(3):
                if r:
                    sp.wait_ge(round_done, r + 1)
                else:
                    sp.wait_ge(s_v, mark["prepared"])
                with sp.Fori(0, NITER // 2) as pair:
                    for half in range(2):
                        i = pair * 2 + half
                        if r == 1:
                            sp.wait_ge(n_v, i * NV[r] + (FEAT[r] + vb[r]))
                            sp.sem_inc(sp_turn, 1)
                            sp.dma_start(x1_tab.rearrange("(b p) d -> p b d", p=P)[:, bass.ds(i * NB, NB), :], feat)\
                              .then_inc(x1_st, 16)
                        sp.wait_ge(n_v, i * NV[r] + (FEAT[r] + 5 + vb[r]))
                        sp.sem_inc(sp_turn, 1)
                        sp.dma_start(y_tab.rearrange("(b p) c -> p b c", p=P)[:, bass.ds(i * NB, NB), :],
                                     ycols[r][:, bass.ds(i * NB, NB), :]).then_inc(y_st, 16)
                sp.wait_ge(n_v, vb[r + 1])
                if r == 0:
                    for b0, blocks, K, s0 in REG:
                        with sp.Fori(0, blocks // 2) as i:
                            for j in range(2):
                                sp.wait_ge(evacd, i * (2 * WPB) + ((b0 + j + 1) * WPB + 3))
                                sp.sem_inc(sp_turn, 1)
                                sp.dma_start(a_dram[j][bass.ds(i + b0 // 2, 1), :, :, :]
                                             .rearrange("b u p c -> p (b u) c"),
                                             abuf[:, j, :].rearrange("p (u c) -> p u c", u=2)).then_inc(stored[j], 16)
                    sp.wait_ge(round_done, 1)
                    sp.dma_start(dst_rows.bitcast(I32), dst.rearrange("(p c) -> p c", p=TP)).then_inc(s_lde, 16)
                    sp.wait_ge(s_path_in, 32)
                    sp.wait_ge(s_pc, len(jobs))
                    ea = edge_attr.rearrange("(g p j) d -> g p (j d)", p=P, j=EG)
                    with sp.Fori(0, ESTEPS // EB) as i:
                        grp = load(ENG.SP, i * EB + (SPAD + ES * P), EB, GROUPS - 1)
                        for h in range(EB):
                            sp.wait_ge(e_rem[h], i + 1)
                            sp.sem_inc(sp_turn, 1)
                            sp.dma_start(feats[:, h, :, :].rearrange("p j d -> p (j d)"), ea[bass.ds(grp[h], 1), :, :].rearrange("g p c -> (g p) c"))\
                              .then_inc(e_in[h], 16)
                    continue
                with sp.Fori(0, ITERS) as i:
                    for j in range(2):
                        for u in range(2):
                            sp.wait_ge(a_used[j][u], i + (1 + (r - 1) * ITERS))
                            sp.sem_inc(sp_turn, 1)
                            sp.dma_start(abuf[:, j, u * HALF * P:(u + 1) * HALF * P],
                                         a_dram[j][bass.ds(i, 1), u, :, :].rearrange("b p c -> p (b c)"))\
                              .then_inc(a_in[j][u], 16)
            sp.wait_ge(y_st, 16 * NITER * 3)
            sp.wait_ge(s_fin, 7)
            sp.dma_start(out[0:FULL * P, :].rearrange("(b p) d -> p b d", p=P), acc[:, 0:FULL, :]).then_inc(s_out, 16)
            sp.dma_start(out[FULL * P:N, :], acc[0:REST, FULL, :]).then_inc(s_out, 16)
            sp.wait_ge(s_out, 32)


CONSTS = 7
LOADS = 18


_INS = ['x', 'src', 'dst', 'edge_attr_64', 'L0_gnn_W_fc', 'L0_gnn_b_fc', 'L0_gnn_W_res', 'L0_gnn_b_res',
        'L1_gnn_Wm1', 'L1_gnn_bm1', 'L1_gnn_We1', 'L1_gnn_be1', 'L1_gnn_Ws1', 'L1_gnn_bs1',
        'L1_gnn_Wm2', 'L1_gnn_bm2', 'L1_gnn_We2', 'L1_gnn_be2', 'L1_gnn_Ws2', 'L1_gnn_bs2']
_OUTS = [((12500, 64), 'float32')]


def kernel(**inputs):
    import numpy as _np
    import concourse.bacc as _bacc
    from concourse import mybir as _mybir
    from concourse.bass_utils import run_bass_kernel_spmd as _run

    nc = _bacc.Bacc("TRN2", target_bir_lowering=False, num_devices=1)
    arrays, args = {"in_step_constants": step_constants()}, []
    for name in _INS:
        arrays[f"in_{name}_dram"] = _np.ascontiguousarray(inputs[name])
    for name, a in arrays.items():
        args.append(nc.dram_tensor(name, a.shape, _mybir.dt.from_np(a.dtype), kind="ExternalInput").ap())
    for i, (shape, dtype) in enumerate(_OUTS):
        dt = _mybir.dt.from_np(_np.dtype(dtype))
        args.append(nc.dram_tensor(f"out_{i}_dram", shape, dt, kind="ExternalOutput").ap())
    gnn_program(nc, *args)
    r = _run(nc, [arrays], core_ids=[0])
    return r.results[0]["out_0_dram"]
```
